# Optimizing a Trainium2 kernel written in Bass

```python
import numpy as np
import jax
import jax.numpy as jnp

def _softmax(x, axis=-1):
    return jax.nn.softmax(x, axis=axis)

def _gelu(x):
    return jax.nn.gelu(x, approximate=True)

def _silu(x):
    return jax.nn.silu(x)

def _sigmoid(x):
    return jax.nn.sigmoid(x)

def _layernorm(x, axis=-1, eps=1e-05):
    m = jnp.mean(x, axis=axis, keepdims=True)
    v = jnp.var(x, axis=axis, keepdims=True)
    return (x - m) / jnp.sqrt(v + eps)

def _scatter_add(tgt, idx, src, axis=0):
    return tgt.at[idx].add(src)

def _segment_sum(src, seg, n):
    return jax.ops.segment_sum(src, seg, n)
kernel_name = 'mk_prb_d1_jaxref_r2_8f5806'

def setup_inputs(seed: int=0):
    np.random.seed(seed)
    _w = jnp.asarray

    def _L0_attn_setup():
        import jax, jax.numpy as jnp
        import numpy as np
        D_MODEL = 512
        N_HEADS = 64
        D_HEAD = D_MODEL // N_HEADS
        B = 2
        S = 1024

        def _xavier(key, fan):
            lim = np.sqrt(6.0 / (2 * fan)).astype(np.float32)
            return jax.random.uniform(key, (fan, fan), dtype=jnp.float32, minval=-lim, maxval=lim)
        key = jax.random.key(seed)
        ks = jax.random.split(key, 9)
        blim = 1.0 / np.sqrt(D_MODEL)

        def bias(k):
            return jax.random.uniform(k, (D_MODEL,), dtype=jnp.float32, minval=-blim, maxval=blim)
        return {'x': jax.random.normal(ks[0], (B, S, D_MODEL), dtype=jnp.float32), 'Wq': _xavier(ks[1], D_MODEL), 'bq': bias(ks[2]), 'Wk': _xavier(ks[3], D_MODEL), 'bk': bias(ks[4]), 'Wv': _xavier(ks[5], D_MODEL), 'bv': bias(ks[6]), 'Wo': _xavier(ks[7], D_MODEL), 'bo': jnp.zeros((D_MODEL,), dtype=jnp.float32), 'beta': jnp.zeros((1,), dtype=jnp.float32)}
    _L0_attn_in = _L0_attn_setup()

    def _L0_ffn_setup():
        import jax, jax.numpy as jnp
        import numpy as np
        FP8_MAX = 448.0
        key = jax.random.key(seed)
        k_x, k_w, k_b = jax.random.split(key, 3)
        B, S, IN, OUT = (4, 4096, 512, 512)
        x = jax.random.normal(k_x, (B, S, IN), dtype=jnp.float32)
        w_fp32 = jax.random.normal(k_w, (OUT, IN), dtype=jnp.float32)
        weight_fp8 = w_fp32.astype(jnp.float8_e4m3fn).astype(jnp.float32)
        bias = jax.random.normal(k_b, (OUT,), dtype=jnp.float32)
        input_scale = jnp.ones((1,), dtype=jnp.float32)
        weight_scale = jnp.ones((1,), dtype=jnp.float32)
        return {'x': x, 'weight_fp8': weight_fp8, 'bias': bias, 'input_scale': input_scale, 'weight_scale': weight_scale}
    _L0_ffn_in = _L0_ffn_setup()
    _d = {'L0_attn_x': _L0_attn_in['x'], 'L0_attn_Wq': _L0_attn_in['Wq'], 'L0_attn_bq': _L0_attn_in['bq'], 'L0_attn_Wk': _L0_attn_in['Wk'], 'L0_attn_bk': _L0_attn_in['bk'], 'L0_attn_Wv': _L0_attn_in['Wv'], 'L0_attn_bv': _L0_attn_in['bv'], 'L0_attn_Wo': _L0_attn_in['Wo'], 'L0_attn_bo': _L0_attn_in['bo'], 'L0_attn_beta': _L0_attn_in['beta'], 'L0_ffn_weight_fp8': _L0_ffn_in['weight_fp8'], 'L0_ffn_bias': _L0_ffn_in['bias'], 'L0_ffn_input_scale': _L0_ffn_in['input_scale'], 'L0_ffn_weight_scale': _L0_ffn_in['weight_scale']}
    _x0 = _d['L0_attn_x']
    _d['L0_attn_x'] = jax.random.normal(jax.random.fold_in(jax.random.key(seed), 1), (4, 2048, 512), dtype=_x0.dtype)
    del _x0
    return _d

def reference(L0_attn_x, L0_attn_Wq, L0_attn_bq, L0_attn_Wk, L0_attn_bk, L0_attn_Wv, L0_attn_bv, L0_attn_Wo, L0_attn_bo, L0_attn_beta, L0_ffn_weight_fp8, L0_ffn_bias, L0_ffn_input_scale, L0_ffn_weight_scale):

    def _L0_attn_ref(x, Wq, bq, Wk, bk, Wv, bv, Wo, bo, beta):
        import jax, jax.numpy as jnp
        import numpy as np
        D_MODEL = 512
        N_HEADS = 64
        D_HEAD = D_MODEL // N_HEADS
        B = 2
        S = 1024

        def _xavier(key, fan):
            lim = np.sqrt(6.0 / (2 * fan)).astype(np.float32)
            return jax.random.uniform(key, (fan, fan), dtype=jnp.float32, minval=-lim, maxval=lim)
        b, s, dm = x.shape
        h, d = (N_HEADS, D_HEAD)

        def heads(y):
            return y.reshape(b, s, h, d).transpose(0, 2, 1, 3).reshape(b * h, s, d)
        q = heads(x @ Wq.T + bq)
        k = heads(x @ Wk.T + bk)
        v = heads(x @ Wv.T + bv)
        be = jnp.exp(beta)
        q = jax.nn.softmax(be * q, axis=-1)
        k = jax.nn.softmax(be * k, axis=-1)
        kv = jnp.cumsum(jnp.einsum('zsD,zsd->zsDd', k, v), axis=1)
        kn = jnp.cumsum(k, axis=1)
        num = jnp.einsum('zsD,zsDd->zsd', q, kv)
        den = jnp.sum(q * kn, axis=-1, keepdims=True)
        out = num / den
        out = out.reshape(b, h, s, d).transpose(0, 2, 1, 3).reshape(b, s, dm)
        return out @ Wo.T + bo

    def _L0_ffn_ref(x, weight_fp8, bias, input_scale, weight_scale):
        import jax, jax.numpy as jnp
        import numpy as np
        FP8_MAX = 448.0
        x_q = jnp.clip(x / input_scale, -FP8_MAX, FP8_MAX)
        x_dq = x_q.astype(jnp.float8_e4m3fn).astype(x.dtype) * input_scale
        w_dq = weight_fp8 * weight_scale
        out = jnp.einsum('bsi,oi->bso', x_dq, w_dq) + bias
        return out
    x = L0_attn_x
    xn = _layernorm(x, axis=-1)
    x = x + _L0_attn_ref(xn, L0_attn_Wq, L0_attn_bq, L0_attn_Wk, L0_attn_bk, L0_attn_Wv, L0_attn_bv, L0_attn_Wo, L0_attn_bo, L0_attn_beta) + _L0_ffn_ref(xn, L0_ffn_weight_fp8, L0_ffn_bias, L0_ffn_input_scale, L0_ffn_weight_scale)
    return x

_drawn_inputs = setup_inputs


def setup_inputs(seed=0):
    import zlib

    import numpy as np

    out = dict(_drawn_inputs(seed))
    spreads = {'L0_attn_bo': (0.0, 0.8)}
    factors = {'L0_attn_Wq': 8.0,
     'L0_attn_bq': 24.819,
     'L0_attn_Wk': 8.0,
     'L0_attn_bk': 27.858,
     'L0_attn_Wv': 8.0,
     'L0_attn_bv': 8.0,
     'L0_attn_Wo': 8.0}
    for name, (base, spread) in spreads.items():
        noise = np.random.default_rng([zlib.crc32(name.encode()), seed]).standard_normal(out[name].shape)
        drawn = base * np.exp(spread * noise) if base else spread * noise
        out[name] = jnp.asarray(drawn.astype(out[name].dtype))
    for name, factor in factors.items():
        out[name] = (out[name] * factor).astype(out[name].dtype)
    return out
```

```python
from contextlib import ExitStack

import numpy as np
import concourse.bass as bass
import concourse.mybir as mybir

F32 = mybir.dt.float32
F16 = mybir.dt.float16
BF16 = mybir.dt.bfloat16
I32 = mybir.dt.int32
ALU = mybir.AluOpType
ACT = mybir.ActivationFunctionType
AX = mybir.AxisListType

P = 128
SEQS = 4
TOK = P // SEQS
LEN = 2048
DM = 512
HEADS = 64
DH = DM // HEADS
J = 4
G = HEADS // J
KC = DM // P
STEPS = LEN // TOK
PEELED = 3
VW = DH + 1
GW = SEQS * VW
EPS = 1e-5
FP8_MAX = 448.0
FP8_MIN_NORMAL = 2.0 ** -6
ROUND_TO_4_BITS = 1.5 * 2.0 ** 20
EXPONENT = 0x7F800000
RSQRT_GUESS = 0x5F3759DF
NEWTON = 3
MATRICES = 5
MQ, MK, MV, MO, MF = range(MATRICES)
C_ID = 0
C_HEAD = C_ID + P
C_SEQ = C_HEAD + J
C_TRI = C_SEQ + SEQS
C_PART = C_TRI + TOK
C_ALL = C_PART + 3


class Step:

    def __init__(self, k, off):
        self.k, self.off = k, off

    def __add__(self, n):
        return Step(self.k, self.off + n)

    def __sub__(self, n):
        return self + (-n)

    @property
    def n(self):
        return self.k * 2 + self.off

    @property
    def parity(self):
        return self.off % 2

    @property
    def half(self):
        return self.k + self.off // 2

    def exists(self):
        return not isinstance(self.k, int) or 0 <= self.off < STEPS

    def after(self, n):
        return not isinstance(self.k, int) or self.off >= n


def iterations(eng, body):
    for i in range(-1, PEELED):
        body(Step(0, i))
    with eng.Fori(0, (STEPS - 1 - PEELED) // 2) as k:
        body(Step(k, PEELED))
        body(Step(k, PEELED + 1))
    body(Step(0, STEPS - 1))
    body(Step(0, STEPS))


def build(nc, x, wq, bq, wk, bk, wv, bv, wo, bo, beta, wf, bf, in_scale, w_scale, const, out):
    x_t = x.rearrange("b (t s) d -> t b s d", s=TOK)
    out_t = out.rearrange("b (t s) d -> t b s d", s=TOK)

    with ExitStack() as ctx:
        def sb(name, shape, dt=F32):
            return ctx.enter_context(nc.sbuf_tensor(name, shape, dt))

        def ps(name, cols):
            return ctx.enter_context(nc.psum_tensor(name, [P, cols], F32))

        def sem(name):
            return ctx.enter_context(nc.semaphore(name))

        cst = sb("cst", [P, C_ALL])
        ident = cst[:, C_ID:C_ID + P]
        head_mask = cst[:, C_HEAD:C_HEAD + J]
        seq_mask = cst[:, C_SEQ:C_SEQ + SEQS]
        tri = cst[:, C_TRI:C_TRI + TOK]
        part_mask = cst[0:3, C_PART:C_PART + 3]
        w_hi = sb("w_hi", [P, MATRICES, KC, DM], F16)
        w_lo = sb("w_lo", [P, MATRICES, KC, DM], F16)
        w_nat = [sb(f"w_nat{n}", [P, KC, DM]) for n in range(2)]
        bias_raw = sb("bias_raw", [3, 5, DM])
        bias_res = sb("bias_res", [3, 2, DM])
        bias_part = sb("bias_part", [3, 3, DM], BF16)
        bias_sum = sb("bias_sum", [3, 2, DM])
        bias_rows = sb("bias_rows", [3, 4, DM], BF16)
        ones3 = sb("ones3", [3, P], BF16)
        scal = sb("scal", [P, 3])
        amax = sb("amax", [P, MATRICES])
        amax_all = sb("amax_all", [P, MATRICES])
        w_top = sb("w_top", [P, MATRICES])
        w_scale_up = sb("w_scale_up", [P, MATRICES])
        w_scale_dn = sb("w_scale_dn", [P, MATRICES])
        w_mult = sb("w_mult", [P, MATRICES])
        misc = sb("misc", [P, 10])
        both_scales = misc[:, 0:1]
        exp_beta = misc[:, 1:2]
        q_exp_scale = misc[:, 2:3]
        k_exp_scale = misc[:, 3:4]
        out_up = misc[:, 4:5]
        out_dn = misc[:, 5:6]
        in_inv = misc[:, 6:7]
        tmp1 = misc[:, 7:8]
        tmp2 = misc[:, 8:9]
        abs_scales = misc[:, 9:10]
        x_in = sb("x_in", [P, 2, DM])
        x_res = sb("x_res", [P, 2, DM])
        stats = sb("stats", [P, 6])
        mv = sb("mv", [P, 2])
        var_e = sb("var_e", [P, 1])
        shifted = sb("shifted", [P, 1], I32)
        rstd = sb("rstd", [P, NEWTON + 1])
        nsq = sb("nsq", [P, NEWTON])
        nhalf = sb("nhalf", [P, NEWTON])
        xn = sb("xn", [P, DM])
        xh = sb("xh", [P, KC, P], F16)
        xl = sb("xl", [P, KC, P], F16)
        y = sb("y", [P, DM])
        y_exp = sb("y_exp", [P, DM])
        y_magic = sb("y_magic", [P, DM])
        y_sum = sb("y_sum", [P, DM])
        y_round = sb("y_round", [P, DM])
        xq = sb("xq", [P, 2, KC, P], F16)
        q_max = sb("q_max", [P, HEADS])
        k_max = sb("k_max", [P, HEADS])
        k_sum = sb("k_sum", [P, HEADS])
        k_rec = sb("k_rec", [P, HEADS])
        q_shift = sb("q_shift", [P, DM])
        k_shift = sb("k_shift", [P, DM])
        q_e = sb("q_e", [P, DM])
        k_e = sb("k_e", [P, DM])
        k_n = sb("k_n", [P, 2, DM])
        qT = sb("qT", [P, G, TOK])
        kT = sb("kT", [P, G, TOK])
        q_heads = sb("q_heads", [P, 2, G, J, TOK])
        k_seqs = sb("k_seqs", [P, G, SEQS, TOK])
        v_seqs = sb("v_seqs", [P, 2, HEADS, SEQS, VW])
        att = sb("att", [P, G, J, TOK])
        st_masked = sb("st_masked", [P, G, J, VW])
        st_step = sb("st_step", [P, G, VW])
        st_run = sb("st_run", [P, G, VW])
        st_seqs = sb("st_seqs", [P, 2, G, SEQS, VW])
        den_rec = sb("den_rec", [P, 2, G // 2 * SEQS])
        a_n = sb("a_n", [P, SEQS, G, DH])
        ah = sb("ah", [P, J, P], F16)
        al = sb("al", [P, J, P], F16)
        o_sb = sb("o_sb", [P, 2, DM])
        q_ps = ps("q_ps", DM)
        k_ps = ps("k_ps", DM)
        vo_ps = ps("vo_ps", DM)
        t_ps = ps("t_ps", DM)
        s_ps = ps("s_ps", 2 * DM)
        a_ps = ps("a_ps", 2 * DM)
        s_state = s_ps[:, :].rearrange("p (n w) -> p n w", n=2)[:, :, 0:G // 2 * J * VW]
        a_view = a_ps[:, :].rearrange("p (n w) -> p n w", n=2)[:, :, 0:G // 2 * GW]
        setup_banks = [q_ps, k_ps, vo_ps, t_ps]

        c_loaded, b_loaded, m_loaded = sem("c_loaded"), sem("b_loaded"), sem("m_loaded")
        w_loaded = [sem("w_loaded0"), sem("w_loaded1")]
        amax_ready, amax_shared = sem("amax_ready"), sem("amax_shared")
        chain = sem("chain")
        mult_ready, beta_exped = sem("mult_ready"), sem("beta_exped")
        wt_done, wh_ready, wl_ready = sem("wt_done"), sem("wh_ready"), sem("wl_ready")
        ones_ready, setup_done = sem("ones_ready"), sem("setup_done")
        x_loaded = [sem("x_loaded0"), sem("x_loaded1")]
        r_loaded = [sem("r_loaded0"), sem("r_loaded1")]
        stored = [sem("stored0"), sem("stored1")]
        stats_ready, mv_ready, rstd_ready = sem("stats_ready"), sem("mv_ready"), sem("rstd_ready")
        xn_ready, xT_done, xh_ready, xl_ready = sem("xn_ready"), sem("xT_done"), sem("xh_ready"), sem("xl_ready")
        y_ready, yexp_ready, magic_ready = sem("y_ready"), sem("yexp_ready"), sem("magic_ready")
        ysum_ready, yround_ready, xq_ready = sem("ysum_ready"), sem("yround_ready"), sem("xq_ready")
        q_done, k_done, v_done = sem("q_done"), sem("k_done"), sem("v_done")
        qmax_ready, qshift_ready, qe_ready = sem("qmax_ready"), sem("qshift_ready"), sem("qe_ready")
        kmax_ready, kshift_ready, ke_ready = sem("kmax_ready"), sem("kshift_ready"), sem("ke_ready")
        ksum_ready, krec_ready, kn_ready = sem("ksum_ready"), sem("krec_ready"), sem("kn_ready")
        qT_ready, kT_ready = sem("qT_ready"), sem("kT_ready")
        qheads_ready, kseqs_ready, vseqs_ready = sem("qheads_ready"), sem("kseqs_ready"), sem("vseqs_ready")
        scores_done, att_ready = sem("scores_done"), sem("att_ready")
        state_done, masked_ready, ststep_ready = sem("state_done"), sem("masked_ready"), sem("ststep_ready")
        strun_ready, stseqs_ready = sem("strun_ready"), sem("stseqs_ready")
        a_done, rec_ready, an_ready = sem("a_done"), sem("rec_ready"), sem("an_ready")
        aT_done, ah_ready, al_ready = sem("aT_done"), sem("ah_ready"), sem("al_ready")
        dve_waited, pe_waited = sem("dve_waited"), sem("pe_waited")
        f_done, o_done, o_ready = sem("f_done"), sem("o_done"), sem("o_ready")

        block = ctx.enter_context(nc.Block())

        weights = [wq, wk, wv, wo, wf]
        turn = [MQ, MK, MV, MF, MO]
        loads = list(range(MATRICES)) + turn[:-1]
        wo_kept = att[:, :, :, :].rearrange("p g j s -> p (g j s)")\
            .rearrange("p (c n) -> p c n", c=KC)

        @block.sync
        def _(sp):
            sp.dma_start(cst[:, :], const).then_inc(c_loaded, 16)
            for n, s in enumerate((beta, in_scale, w_scale)):
                sp.dma_start(scal[:, n:n + 1], s.rearrange("(a n) -> a n", a=1).to_broadcast([P, 1]))\
                    .then_inc(m_loaded, 16)
            for n, b in enumerate((bq, bk, bv, bo, bf)):
                sp.dma_start(bias_raw[:, n, :], b.rearrange("(a n) -> a n", a=1).to_broadcast([3, DM]))\
                    .then_inc(b_loaded, 16)
            for r, m in enumerate(loads):
                if 2 <= r < MATRICES + 2:
                    sp.wait_ge(amax_ready, min(r - 1, MATRICES))
                if r >= MATRICES + 2:
                    sp.wait_ge(wt_done, KC * (r - 1 - MATRICES))
                sp.dma_start(w_nat[r % 2][:, :, :], weights[m].rearrange("(c p) d -> p c d", p=P))\
                    .then_inc(w_loaded[r % 2], 16)

            def load_x(t):
                if t.after(2):
                    sp.wait_ge(xn_ready, (t - 1).n)
                sp.dma_start(x_in[:, t.parity, :], x_t[t.n]).then_inc(x_loaded[t.parity], 16)

            def body(i):
                if (i + 1).exists():
                    load_x(i + 1)
                if i.exists():
                    if i.after(2):
                        sp.wait_ge(o_ready, (i - 1).n)
                    sp.dma_start(x_res[:, i.parity, :], x_t[i.n]).then_inc(r_loaded[i.parity], 16)

            iterations(sp, body)
            for n in range(2):
                sp.wait_ge(stored[n], 16 * (STEPS // 2))

        @block.gpsimd
        def _(pool):
            pool.wait_ge(amax_ready, MATRICES)
            nc.gpsimd.partition_all_reduce(amax_all[:, :], amax[:, :], P, bass.bass_isa.ReduceOp.max)\
                .then_inc(amax_shared, 1)
            pool.wait_ge(c_loaded, 16)

            def body(i):
                if i.exists():
                    pool.wait_ge(kT_ready, (i + 1).n)
                    if i.after(1):
                        pool.wait_ge(scores_done, i.n * 4)
                    nc.gpsimd.tensor_tensor(
                        k_seqs[:, :, :, :], kT[:, :, None, :].to_broadcast([P, G, SEQS, TOK]),
                        seq_mask[:, None, :, None].to_broadcast([P, G, SEQS, TOK]), ALU.mult)\
                        .then_inc(kseqs_ready, 1)
                t = i + 1
                if t.exists():
                    pool.wait_ge(y_ready, (t + 1).n)
                    pool.wait_ge(magic_ready, (t + 1).n)
                    nc.gpsimd.tensor_tensor(y_sum[:, :], y[:, :], y_magic[:, :], ALU.add)\
                        .then_inc(ysum_ready, 1)
                    pool.wait_ge(ysum_ready, (t + 1).n)
                    if t.after(1):
                        pool.wait_ge(xq_ready, t.n)
                    nc.gpsimd.tensor_tensor(y_round[:, :], y_sum[:, :], y_magic[:, :], ALU.subtract)\
                        .then_inc(yround_ready, 1)

            iterations(pool, body)

        @block.scalar
        def _(act):
            act.wait_ge(m_loaded, 48)
            nc.scalar.activation(exp_beta, scal[:, 0:1], ACT.Exp).then_inc(beta_exped, 1)
            act.wait_ge(mult_ready, 1)
            for n in range(MATRICES * KC):
                m, c = turn[n // KC], n % KC
                act.wait_ge(wt_done, n + 1)
                nc.scalar.activation(w_hi[:, m, c, :], setup_banks[n % 4][:, :], ACT.Copy,
                                     scale=w_mult[:, m:m + 1]).then_inc(wh_ready, 1)
            act.wait_ge(setup_done, 1)

            def body(i):
                if i.exists():
                    act.wait_ge(qshift_ready, (i + 1).n)
                    if i.after(1):
                        act.wait_ge(qT_ready, i.n)
                    nc.scalar.activation(q_e[:, :], q_shift[:, :], ACT.Exp, scale=q_exp_scale)\
                        .then_inc(qe_ready, 1)
                    act.wait_ge(kshift_ready, (i + 1).n)
                    if i.after(1):
                        act.wait_ge(kn_ready, i.n)
                    nc.scalar.activation(k_e[:, :], k_shift[:, :], ACT.Exp, scale=k_exp_scale)\
                        .then_inc(ke_ready, 1)
                    act.wait_ge(v_done, (i + 1).n)
                    if i.after(2):
                        act.wait_ge(a_done, (i - 1).n)
                    for b in range(SEQS):
                        last = nc.scalar.activation(
                            v_seqs[:, i.parity, :, b, 0:DH],
                            vo_ps[:, :].rearrange("p (h d) -> p h d", d=DH),
                            ACT.Copy, scale=seq_mask[:, b:b + 1])
                    last.then_inc(vseqs_ready, 1)
                    act.wait_ge(qT_ready, (i + 1).n)
                    for j in range(J):
                        last = nc.scalar.activation(q_heads[:, i.parity, :, j, :], qT[:, :, :],
                                                    ACT.Copy, scale=head_mask[:, j:j + 1])
                    last.then_inc(qheads_ready, 1)
                t = i + 1
                if t.exists():
                    act.wait_ge(xT_done, (t + 1).n)
                    if t.after(1):
                        act.wait_ge(v_done, t.n)
                    nc.scalar.activation(xh[:, :, :].rearrange("p c s -> p (c s)"), t_ps[:, :],
                                         ACT.Copy).then_inc(xh_ready, 1)
                    if t.after(1):
                        act.wait_ge(yround_ready, t.n)
                        act.wait_ge(magic_ready, t.n)
                    nc.scalar.activation(y[:, :], t_ps[:, :], ACT.Copy, scale=in_inv)\
                        .then_inc(y_ready, 1)
                t = i - 1
                if t.exists():
                    act.wait_ge(aT_done, (t + 1).n)
                    if t.after(1):
                        act.wait_ge(o_done, t.n)
                    nc.scalar.activation(ah[:, :, :].rearrange("p j s -> p (j s)"), t_ps[:, :],
                                         ACT.Copy).then_inc(ah_ready, 1)
                    act.wait_ge(o_ready, (t + 1).n)
                    act.dma_start(out_t[t.n], o_sb[:, t.parity, :]).then_inc(stored[t.parity], 16)

            iterations(act, body)

        @block.vector
        def _(dve):
            links = [0]

            def link(instruction):
                instruction.then_inc(chain, 1)
                links[0] += 1
                dve.wait_ge(chain, links[0])

            v = nc.vector
            v.memset(ones3[:, :], 1.0).then_inc(ones_ready, 1)
            link(v.memset(st_run[:, :, :], 0.0))
            link(v.memset(st_seqs[:, 0, :, :, :], 0.0))
            dve.wait_ge(c_loaded, 16)
            for n in range(2):
                link(v.tensor_copy(v_seqs[:, n, :, :, DH],
                                   seq_mask[:, None, :].to_broadcast([P, HEADS, SEQS])))
            for r in range(MATRICES):
                dve.wait_ge(w_loaded[r % 2], 16 * (r // 2 + 1))
                if r == MO:
                    for oc in range(KC):
                        v.tensor_copy(wo_kept[:, oc, :].rearrange("p (j g d) -> p j g d", j=J, d=DH),
                                      w_nat[r % 2][:, oc, :].rearrange("p (g j d) -> p j g d", j=J, d=DH))
                v.tensor_reduce(amax[:, r:r + 1], w_nat[r % 2][:, :, :], AX.XY, ALU.max,
                                apply_absolute_value=True).then_inc(amax_ready, 1)
            dve.wait_ge(m_loaded, 48)
            link(v.tensor_tensor(both_scales, scal[:, 1:2], scal[:, 2:3], ALU.mult))
            link(v.tensor_scalar(tmp1, both_scales, -1.0, None, ALU.mult))
            link(v.tensor_tensor(abs_scales, both_scales, tmp1, ALU.max))
            dve.wait_ge(amax_shared, 1)
            link(v.tensor_tensor(amax_all[:, MF:MF + 1], amax_all[:, MF:MF + 1], abs_scales, ALU.mult))
            link(v.tensor_scalar(amax_all[:, :], amax_all[:, :], 1e-18, 1e18, ALU.max, ALU.min))
            link(v.tensor_scalar(w_top[:, :].bitcast(I32), amax_all[:, :].bitcast(I32), EXPONENT, None,
                                 ALU.bitwise_and))
            link(v.tensor_scalar(w_scale_dn[:, :], w_top[:, :], 2.0, None, ALU.mult))
            link(v.reciprocal(w_scale_up[:, :], w_scale_dn[:, :]))
            link(v.tensor_tensor(tmp1, w_scale_up[:, MO:MO + 1], w_scale_up[:, MV:MV + 1], ALU.mult))
            link(v.tensor_tensor(out_up, tmp1, w_scale_up[:, MF:MF + 1], ALU.min))
            link(v.reciprocal(out_dn, out_up))
            link(v.tensor_copy(w_mult[:, 0:MO], w_scale_up[:, 0:MO]))
            link(v.tensor_tensor(w_mult[:, MO:MO + 1], out_up, w_scale_dn[:, MV:MV + 1], ALU.mult))
            v.tensor_tensor(w_mult[:, MF:MF + 1], both_scales, out_up, ALU.mult).then_inc(mult_ready, 1)
            link(v.reciprocal(tmp2, scal[:, 1:2]))
            link(v.tensor_scalar(in_inv, tmp2, 1e30, -1e30, ALU.min, ALU.max))
            dve.wait_ge(beta_exped, 1)
            link(v.tensor_tensor(q_exp_scale, exp_beta, w_scale_dn[:, MQ:MQ + 1], ALU.mult))
            link(v.tensor_tensor(k_exp_scale, exp_beta, w_scale_dn[:, MK:MK + 1], ALU.mult))
            dve.wait_ge(b_loaded, 16 * 5)
            link(v.tensor_tensor(bias_raw[:, 3, :], bias_raw[:, 3, :], bias_raw[:, 4, :], ALU.add))
            for m in range(4):
                up = (w_scale_up[0:3, m:m + 1] if m < 3 else out_up[0:3, :])
                link(v.tensor_scalar(bias_raw[:, m, :], bias_raw[:, m, :], up, None, ALU.mult))
                link(v.tensor_copy(bias_part[:, 0, :], bias_raw[:, m, :]))
                link(v.tensor_tensor(bias_res[:, 0, :], bias_raw[:, m, :], bias_part[:, 0, :], ALU.subtract))
                link(v.tensor_copy(bias_part[:, 1, :], bias_res[:, 0, :]))
                link(v.tensor_tensor(bias_res[:, 1, :], bias_res[:, 0, :], bias_part[:, 1, :], ALU.subtract))
                link(v.tensor_copy(bias_part[:, 2, :], bias_res[:, 1, :]))
                link(v.tensor_scalar(bias_sum[:, 0, :], bias_part[:, 0, :], part_mask[:, 0:1], None, ALU.mult))
                link(v.scalar_tensor_tensor(bias_sum[:, 1, :], bias_part[:, 1, :], part_mask[:, 1:2],
                                            bias_sum[:, 0, :], ALU.mult, ALU.add))
                link(v.scalar_tensor_tensor(bias_rows[:, m, :], bias_part[:, 2, :], part_mask[:, 2:3],
                                            bias_sum[:, 1, :], ALU.mult, ALU.add))
            dve.wait_ge(mult_ready, 1)
            for n in range(MATRICES * KC):
                m, c = turn[n // KC], n % KC
                dve.wait_ge(wh_ready, n + 1)
                v.scalar_tensor_tensor(w_lo[:, m, c, :], setup_banks[n % 4][:, :], w_mult[:, m:m + 1],
                                       w_hi[:, m, c, :], ALU.mult, ALU.subtract).then_inc(wl_ready, 1)
            dve.wait_ge(wl_ready, MATRICES * KC)
            v.tensor_copy(tmp1, tmp2).then_inc(setup_done, 1)

            def heads(ap):
                return ap.rearrange("p (h d) -> p h d", d=DH)

            def per_head(ap):
                return ap[:, :, None].to_broadcast([P, HEADS, DH])

            def normalise(t):
                dve.wait_ge(x_loaded[t.parity], (t + 2).half * 16)
                v.bn_stats(stats[:, :], x_in[:, t.parity, :]).then_inc(stats_ready, 1)
                dve.wait_ge(stats_ready, (t + 1).n)
                dve.sem_inc(dve_waited, 1)
                v.bn_aggr(mv[:, :], stats[:, :]).then_inc(mv_ready, 1)
                dve.wait_ge(mv_ready, (t + 1).n)
                done = t.n * (3 + 3 * NEWTON)

                def root_step(n, instruction):
                    instruction.then_inc(rstd_ready, 1)
                    dve.wait_ge(rstd_ready, done + n)

                root_step(1, v.tensor_scalar(var_e[:, :], mv[:, 1:2], EPS, None, ALU.add))
                root_step(2, v.tensor_scalar(shifted[:, :], var_e[:, :].bitcast(I32), 1, None,
                                             ALU.logical_shift_right))
                root_step(3, v.tensor_scalar(rstd[:, 0:1].bitcast(I32), shifted[:, :], -1, RSQRT_GUESS,
                                             ALU.mult, ALU.add))
                for n in range(NEWTON):
                    r = rstd[:, n:n + 1]
                    root_step(3 * n + 4, v.tensor_tensor(nsq[:, n:n + 1], r, r, ALU.mult))
                    root_step(3 * n + 5, v.tensor_scalar(nhalf[:, n:n + 1], nsq[:, n:n + 1],
                                                         var_e[:, :], -0.5, ALU.mult, ALU.mult))
                    root_step(3 * n + 6, v.scalar_tensor_tensor(rstd[:, n + 1:n + 2], nhalf[:, n:n + 1],
                                                                1.5, r, ALU.add, ALU.mult))
                if t.after(1):
                    dve.wait_ge(xT_done, t.n)
                v.tensor_scalar(xn[:, :], x_in[:, t.parity, :], mv[:, 0:1], rstd[:, NEWTON:NEWTON + 1],
                                ALU.subtract, ALU.mult).then_inc(xn_ready, 1)

            def shift(i, ps_, done, mx, mx_ready, sh, sh_ready, read):
                dve.wait_ge(done, (i + 1).n)
                v.tensor_reduce(mx[:, :], heads(ps_[:, :]), AX.X, ALU.max).then_inc(mx_ready, 1)
                dve.wait_ge(mx_ready, (i + 1).n)
                if i.after(1):
                    dve.wait_ge(read, i.n)
                v.tensor_tensor(heads(sh[:, :]), heads(ps_[:, :]), per_head(mx[:, :]), ALU.subtract)\
                    .then_inc(sh_ready, 1)

            def state(i):
                dve.wait_ge(state_done, i.n)
                for n in range(2):
                    half = slice(n * G // 2, (n + 1) * G // 2)
                    last = v.tensor_tensor(
                        st_masked[:, half, :, :],
                        s_state[:, n, :].rearrange("p (g j w) -> p g j w", j=J, w=VW),
                        head_mask[:, None, :, None].to_broadcast([P, G // 2, J, VW]), ALU.mult)
                last.then_inc(masked_ready, 1)
                dve.wait_ge(masked_ready, i.n)
                v.tensor_reduce(st_step[:, :, :], st_masked[:, :, :, :].rearrange("p g j w -> p g w j"),
                                AX.X, ALU.add).then_inc(ststep_ready, 1)
                dve.wait_ge(ststep_ready, i.n)
                v.tensor_tensor(st_run[:, :, :], st_run[:, :, :], st_step[:, :, :], ALU.add)\
                    .then_inc(strun_ready, 1)
                dve.wait_ge(strun_ready, i.n)
                if i.after(2):
                    dve.wait_ge(a_done, (i - 1).n)
                v.tensor_tensor(st_seqs[:, i.parity, :, :, :],
                                st_run[:, :, None, :].to_broadcast([P, G, SEQS, VW]),
                                seq_mask[:, None, :, None].to_broadcast([P, G, SEQS, VW]), ALU.mult)\
                    .then_inc(stseqs_ready, 1)

            def mask_scores(i, c):
                dve.wait_ge(scores_done, i.n * 4 + c + 1)
                if c == 0 and i.after(1):
                    dve.wait_ge(a_done, i.n)
                v.tensor_tensor(att[:, 4 * c:4 * c + 4, :, :].rearrange("p g j s -> p (g j) s"),
                                s_ps[:, DM * (c % 2):DM * (c % 2 + 1)].rearrange("p (h s) -> p h s", s=TOK),
                                tri[:, None, :].to_broadcast([P, 4 * J, TOK]), ALU.mult)\
                    .then_inc(att_ready, 1)

            def body(i):
                t = i + 1
                if t.exists():
                    normalise(t)
                if i.exists():
                    shift(i, q_ps, q_done, q_max, qmax_ready, q_shift, qshift_ready, qe_ready)
                    shift(i, k_ps, k_done, k_max, kmax_ready, k_shift, kshift_ready, ke_ready)
                    dve.wait_ge(qe_ready, (i + 1).n)
                    if i.after(1):
                        dve.wait_ge(qheads_ready, i.n)
                    v.transpose(qT[:, :, :].rearrange("p g s -> p (g s)"), q_e[:, :]).then_inc(qT_ready, 1)
                    dve.wait_ge(ke_ready, (i + 1).n)
                    v.tensor_reduce(k_sum[:, :], heads(k_e[:, :]), AX.X, ALU.add).then_inc(ksum_ready, 1)
                    dve.wait_ge(ksum_ready, (i + 1).n)
                    v.reciprocal(k_rec[:, :], k_sum[:, :]).then_inc(krec_ready, 1)
                    dve.wait_ge(krec_ready, (i + 1).n)
                    if i.after(2):
                        dve.wait_ge(state_done, (i - 1).n)
                    v.tensor_tensor(heads(k_n[:, i.parity, :]), heads(k_e[:, :]), per_head(k_rec[:, :]),
                                    ALU.mult).then_inc(kn_ready, 1)
                    dve.wait_ge(kn_ready, (i + 1).n)
                    if i.after(1):
                        dve.wait_ge(kseqs_ready, i.n)
                    v.transpose(kT[:, :, :].rearrange("p g s -> p (g s)"), k_n[:, i.parity, :])\
                        .then_inc(kT_ready, 1)
                    if i.after(1):
                        state(i)
                t = i - 1
                if t.exists():
                    dve.wait_ge(a_done, (t + 1).n)
                    for n in range(2):
                        a_n_ps = a_view[:, n, :].rearrange("p (m w) -> p m w", w=VW)
                        last = v.reciprocal(den_rec[:, n, :], a_n_ps[:, :, DH])
                    last.then_inc(rec_ready, 1)
                    dve.wait_ge(rec_ready, (t + 1).n)
                    if t.after(1):
                        dve.wait_ge(aT_done, t.n)
                    for n in range(2):
                        a_n_ps = a_view[:, n, :].rearrange("p (g b w) -> p g b w", b=SEQS, w=VW)
                        rec = den_rec[:, n, :].rearrange("p (g b) -> p g b", b=SEQS)
                        last = v.tensor_tensor(
                            a_n[:, :, n * G // 2:(n + 1) * G // 2, :].rearrange("p b g d -> p g b d"),
                            a_n_ps[:, :, :, 0:DH],
                            rec[:, :, :, None].to_broadcast([P, G // 2, SEQS, DH]), ALU.mult)
                    last.then_inc(an_ready, 1)
                t = i + 1
                if t.exists():
                    dve.wait_ge(xh_ready, (t + 1).n)
                    dve.wait_ge(y_ready, (t + 1).n)
                    v.tensor_tensor(xl[:, :, :].rearrange("p c s -> p (c s)"), t_ps[:, :],
                                    xh[:, :, :].rearrange("p c s -> p (c s)"), ALU.subtract)\
                        .then_inc(xl_ready, 1)
                    v.tensor_scalar(y_exp[:, :].bitcast(I32), y[:, :].bitcast(I32), EXPONENT, None,
                                    ALU.bitwise_and).then_inc(yexp_ready, 1)
                    dve.wait_ge(yexp_ready, (t + 1).n)
                    if t.after(1):
                        dve.wait_ge(yround_ready, t.n)
                    v.tensor_scalar(y_magic[:, :], y_exp[:, :], FP8_MIN_NORMAL, ROUND_TO_4_BITS,
                                    ALU.max, ALU.mult).then_inc(magic_ready, 1)
                if i.exists():
                    mask_scores(i, 0)
                    mask_scores(i, 1)
                t = i - 1
                if t.exists():
                    dve.wait_ge(ah_ready, (t + 1).n)
                    v.tensor_tensor(al[:, :, :].rearrange("p j s -> p (j s)"), t_ps[:, :],
                                    ah[:, :, :].rearrange("p j s -> p (j s)"), ALU.subtract)\
                        .then_inc(al_ready, 1)
                if i.exists():
                    mask_scores(i, 2)
                    mask_scores(i, 3)
                t = i + 1
                if t.exists():
                    dve.wait_ge(yround_ready, (t + 1).n)
                    if t.after(2):
                        dve.wait_ge(f_done, (t - 1).n)
                    v.tensor_scalar(xq[:, t.parity, :, :].rearrange("p c s -> p (c s)"), y_round[:, :],
                                    FP8_MAX, -FP8_MAX, ALU.min, ALU.max).then_inc(xq_ready, 1)
                t = i - 1
                if t.exists():
                    dve.wait_ge(o_done, (t + 1).n)
                    dve.wait_ge(r_loaded[t.parity], (t + 2).half * 16)
                    if t.after(2):
                        dve.wait_ge(stored[t.parity], t.half * 16)
                    v.scalar_tensor_tensor(o_sb[:, t.parity, :], vo_ps[:, :], out_dn,
                                           x_res[:, t.parity, :], ALU.mult, ALU.add).then_inc(o_ready, 1)

            iterations(dve, body)

        @block.tensor
        def _(pe):
            mm = nc.tensor.matmul
            pe.wait_ge(c_loaded, 16)
            for k, m in enumerate(turn):
                r = MATRICES + k
                if m == MO:
                    pe.wait_ge(amax_ready, MATRICES)
                else:
                    pe.wait_ge(w_loaded[r % 2], 16 * (r // 2 + 1))
                for c in range(KC):
                    n = k * KC + c
                    if n >= 4:
                        pe.wait_ge(wl_ready, n - 3)
                    for oc in range(KC):
                        src = (wo_kept if m == MO else w_nat[r % 2])[:, oc, c * P:(c + 1) * P]
                        last = nc.tensor.transpose(setup_banks[n % 4][:, oc * P:(oc + 1) * P], src, ident)
                    last.then_inc(wt_done, 1)
            pe.wait_ge(setup_done, 1)
            pe.wait_ge(ones_ready, 1)

            def project(bank, m):
                for c in range(KC):
                    mm(bank[:, :], xh[:, c, :], w_hi[:, m, c, :], start=(c == 0), stop=False)
                    mm(bank[:, :], xh[:, c, :], w_lo[:, m, c, :], start=False, stop=False)
                    mm(bank[:, :], xl[:, c, :], w_hi[:, m, c, :], start=False, stop=False)
                return mm(bank[:, :], ones3[:, :], bias_rows[:, m, :], start=False, stop=True)

            def scores(i, c):
                if c < 2:
                    if i.after(1):
                        pe.wait_ge(masked_ready, i.n)
                else:
                    pe.wait_ge(att_ready, i.n * 4 + c - 1)
                for gg in range(4):
                    g = 4 * c + gg
                    last = mm(s_ps[:, DM * (c % 2) + P * gg:DM * (c % 2) + P * (gg + 1)],
                              k_seqs[:, g, :, :], q_heads[:, i.parity, g, :, :], start=True, stop=True)
                last.then_inc(scores_done, 1)

            def body(i):
                if i.exists():
                    pe.wait_ge(xh_ready, (i + 1).n)
                    pe.wait_ge(xl_ready, (i + 1).n)
                    if i.after(1):
                        pe.wait_ge(qshift_ready, i.n)
                    project(q_ps, MQ).then_inc(q_done, 1)
                    if i.after(1):
                        pe.wait_ge(kshift_ready, i.n)
                    project(k_ps, MK).then_inc(k_done, 1)
                    if i.after(2):
                        pe.wait_ge(o_ready, (i - 1).n)
                    project(vo_ps, MV).then_inc(v_done, 1)
                t = i - 1
                if t.exists() and i.exists():
                    pe.wait_ge(kn_ready, (t + 1).n)
                    pe.wait_ge(vseqs_ready, (t + 1).n)
                    pe.wait_ge(att_ready, (t + 1).n * 4)
                    pe.sem_inc(pe_waited, 1)
                    for g in range(G):
                        col = DM * (g // (G // 2)) + J * VW * (g % (G // 2))
                        for b in range(SEQS):
                            rows = slice(TOK * b, TOK * (b + 1))
                            last = mm(s_ps[rows, col:col + J * VW], k_n[rows, t.parity, TOK * g:TOK * (g + 1)],
                                      v_seqs[rows, t.parity, J * g:J * (g + 1), b, :], start=True, stop=True)
                    last.then_inc(state_done, 1)
                if t.exists():
                    if t.after(1):
                        pe.wait_ge(stseqs_ready, t.n)
                        pe.wait_ge(an_ready, t.n)
                    pe.wait_ge(qheads_ready, (t + 1).n)
                    pe.wait_ge(att_ready, (t + 1).n * 4)
                    pe.wait_ge(vseqs_ready, (t + 1).n)
                    for g in range(G):
                        col = DM * (g // (G // 2)) + GW * (g % (G // 2))
                        mm(a_ps[:, col:col + GW], q_heads[:, t.parity, g, :, :],
                           st_seqs[:, t.parity, g, :, :], start=True, stop=False, skip_group_check=True)
                        for j in range(J):
                            last = mm(a_ps[TOK * j:TOK * (j + 1), col:col + GW], att[:, g, j, :],
                                      v_seqs[:, t.parity, J * g + j, :, :], start=False, stop=True,
                                      skip_group_check=True)
                    last.then_inc(a_done, 1)
                    pe.wait_ge(xq_ready, (t + 1).n)
                    if i.exists():
                        pe.wait_ge(vseqs_ready, (i + 1).n)
                    else:
                        pe.wait_ge(o_ready, t.n)
                    for c in range(KC):
                        mm(vo_ps[:, :], xq[:, t.parity, c, :], w_hi[:, MF, c, :], start=(c == 0), stop=False)
                        mm(vo_ps[:, :], xq[:, t.parity, c, :], w_lo[:, MF, c, :], start=False, stop=False)
                    mm(vo_ps[:, :], ones3[:, :], bias_rows[:, 3, :], start=False, stop=False)\
                        .then_inc(f_done, 1)
                t = i + 1
                if t.exists():
                    pe.wait_ge(xn_ready, (t + 1).n)
                    if t.after(2):
                        pe.wait_ge(ah_ready, (t - 2).n)
                        pe.wait_ge(al_ready, (t - 2).n)
                    for c in range(KC):
                        last = nc.tensor.transpose(t_ps[:, P * c:P * (c + 1)], xn[:, P * c:P * (c + 1)], ident)
                    last.then_inc(xT_done, 1)
                if i.exists():
                    pe.wait_ge(qheads_ready, (i + 1).n)
                    pe.wait_ge(kseqs_ready, (i + 1).n)
                    scores(i, 0)
                    scores(i, 1)
                t = i - 1
                if t.exists():
                    pe.wait_ge(an_ready, (t + 1).n)
                    if (i + 1).exists():
                        pe.wait_ge(xl_ready, (i + 2).n)
                        pe.wait_ge(y_ready, (i + 2).n)
                    for b in range(SEQS):
                        last = nc.tensor.transpose(
                            t_ps[:, :].rearrange("p (j b s) -> p b j s", b=SEQS, s=TOK)[:, b],
                            a_n[:, b, :, :].rearrange("p g d -> p (g d)"), ident)
                    last.then_inc(aT_done, 1)
                if i.exists():
                    scores(i, 2)
                    scores(i, 3)
                if t.exists():
                    pe.wait_ge(ah_ready, (t + 1).n)
                    pe.wait_ge(al_ready, (t + 1).n)
                    for j in range(J):
                        mm(vo_ps[:, :], ah[:, j, :], w_hi[:, MO, j, :], start=False, stop=False)
                        mm(vo_ps[:, :], ah[:, j, :], w_lo[:, MO, j, :], start=False, stop=False)
                        last = mm(vo_ps[:, :], al[:, j, :], w_hi[:, MO, j, :], start=False, stop=(j == J - 1))
                    last.then_inc(o_done, 1)

            iterations(pe, body)


_INS = ["L0_attn_x", "L0_attn_Wq", "L0_attn_bq", "L0_attn_Wk", "L0_attn_bk", "L0_attn_Wv", "L0_attn_bv",
        "L0_attn_Wo", "L0_attn_bo", "L0_attn_beta", "L0_ffn_weight_fp8", "L0_ffn_bias",
        "L0_ffn_input_scale", "L0_ffn_weight_scale"]


def constants():
    c = np.zeros((P, C_ALL), np.float32)
    p = np.arange(P)
    c[:, C_ID:C_ID + P] = np.eye(P)
    c[:, C_HEAD:C_HEAD + J] = (p[:, None] % TOK) // DH == np.arange(J)
    c[:, C_SEQ:C_SEQ + SEQS] = p[:, None] // TOK == np.arange(SEQS)
    c[:, C_TRI:C_TRI + TOK] = p[:, None] % TOK <= np.arange(TOK)
    c[:, C_PART:C_PART + 3] = p[:, None] == np.arange(3)
    return c


def kernel(**inputs):
    import concourse.bacc as bacc
    from concourse.bass_utils import run_bass_kernel_spmd

    nc = bacc.Bacc("TRN2", target_bir_lowering=False, num_devices=1)
    arrays = {name: np.ascontiguousarray(inputs[name]) for name in _INS}
    arrays["const"] = constants()
    args = [nc.dram_tensor(name, a.shape, F32, kind="ExternalInput").ap() for name, a in arrays.items()]
    out = nc.dram_tensor("out", (SEQS, LEN, DM), F32, kind="ExternalOutput").ap()
    build(nc, *args, out)
    r = run_bass_kernel_spmd(nc, [arrays], core_ids=[0])
    return r.results[0]["out"]
```

```python
from contextlib import ExitStack

import numpy as np
import concourse.bass as bass
import concourse.mybir as mybir

F32 = mybir.dt.float32
F16 = mybir.dt.float16
BF16 = mybir.dt.bfloat16
I32 = mybir.dt.int32
ALU = mybir.AluOpType
ACT = mybir.ActivationFunctionType
AX = mybir.AxisListType

P = 128
SEQS = 4
TOK = P // SEQS
LEN = 2048
DM = 512
HEADS = 64
DH = DM // HEADS
J = 4
G = HEADS // J
KC = DM // P
STEPS = LEN // TOK
PEELED = 3
VW = DH + 1
GW = SEQS * VW
EPS = 1e-5
FP8_MAX = 448.0
FP8_MIN_NORMAL = 2.0 ** -6
ROUND_TO_4_BITS = 1.5 * 2.0 ** 20
EXPONENT = 0x7F800000
RSQRT_GUESS = 0x5F3759DF
NEWTON = 3
MATRICES = 5
MQ, MK, MV, MO, MF = range(MATRICES)
C_ID = 0
C_HEAD = C_ID + P
C_SEQ = C_HEAD + J
C_TRI = C_SEQ + SEQS
C_ALL = C_TRI + TOK


class Step:

    def __init__(self, k, off):
        self.k, self.off = k, off

    def __add__(self, n):
        return Step(self.k, self.off + n)

    def __sub__(self, n):
        return self + (-n)

    @property
    def n(self):
        return self.k * 2 + self.off

    @property
    def parity(self):
        return self.off % 2

    @property
    def half(self):
        return self.k + self.off // 2

    def exists(self):
        return not isinstance(self.k, int) or 0 <= self.off < STEPS

    def after(self, n):
        return not isinstance(self.k, int) or self.off >= n


def iterations(eng, body):
    for i in range(-1, PEELED):
        body(Step(0, i))
    with eng.Fori(0, (STEPS - 1 - PEELED) // 2) as k:
        body(Step(k, PEELED))
        body(Step(k, PEELED + 1))
    body(Step(0, STEPS - 1))
    body(Step(0, STEPS))


def build(nc, x, wq, bq, wk, bk, wv, bv, wo, bo, beta, wf, bf, in_scale, w_scale, const, out):
    x_t = x.rearrange("b (t s) d -> t b s d", s=TOK)
    out_t = out.rearrange("b (t s) d -> t b s d", s=TOK)

    with ExitStack() as ctx:
        def sb(name, shape, dt=F32):
            return ctx.enter_context(nc.sbuf_tensor(name, shape, dt))

        def ps(name, cols):
            return ctx.enter_context(nc.psum_tensor(name, [P, cols], F32))

        def sem(name):
            return ctx.enter_context(nc.semaphore(name))

        cst = sb("cst", [P, C_ALL])
        ident = cst[:, C_ID:C_ID + P]
        head_mask = cst[:, C_HEAD:C_HEAD + J]
        seq_mask = cst[:, C_SEQ:C_SEQ + SEQS]
        tri = cst[:, C_TRI:C_TRI + TOK]
        w_hi = sb("w_hi", [P, MATRICES, KC, DM], F16)
        w_lo = sb("w_lo", [P, MATRICES, KC, DM], F16)
        w_nat = [sb(f"w_nat{n}", [P, KC, DM]) for n in range(2)]
        bias = sb("bias", [P, 5, DM])
        scal = sb("scal", [P, 3])
        amax = sb("amax", [P, MATRICES])
        amax_all = sb("amax_all", [P, MATRICES])
        w_top = sb("w_top", [P, MATRICES])
        w_scale_up = sb("w_scale_up", [P, MATRICES])
        w_scale_dn = sb("w_scale_dn", [P, MATRICES])
        w_mult = sb("w_mult", [P, MATRICES])
        misc = sb("misc", [P, 10])
        both_scales = misc[:, 0:1]
        exp_beta = misc[:, 1:2]
        q_exp_scale = misc[:, 2:3]
        k_exp_scale = misc[:, 3:4]
        out_up = misc[:, 4:5]
        out_dn = misc[:, 5:6]
        in_inv = misc[:, 6:7]
        tmp1 = misc[:, 7:8]
        tmp2 = misc[:, 8:9]
        abs_scales = misc[:, 9:10]
        x_in = sb("x_in", [P, 2, DM])
        x_res = sb("x_res", [P, 2, DM])
        stats = sb("stats", [P, 6])
        mv = sb("mv", [P, 2, 2])
        var_e = sb("var_e", [P, 1])
        shifted = sb("shifted", [P, 1], I32)
        minus_half = sb("minus_half", [P, 1])
        three_halves = sb("three_halves", [P, 1])
        guess = sb("guess", [P, 1])
        newton = sb("newton", [P, NEWTON, 4])
        xn = sb("xn", [P, DM])
        xh = sb("xh", [P, KC, P], F16)
        xl = sb("xl", [P, KC, P], F16)
        y = sb("y", [P, DM])
        y_exp = sb("y_exp", [P, DM])
        y_magic = sb("y_magic", [P, DM])
        y_sum = sb("y_sum", [P, DM])
        y_round = sb("y_round", [P, DM])
        xq = sb("xq", [P, 2, KC, P], F16)
        q_max = sb("q_max", [P, HEADS])
        k_max = sb("k_max", [P, HEADS])
        k_sum = sb("k_sum", [P, HEADS])
        k_rec = sb("k_rec", [P, HEADS])
        q_shift = sb("q_shift", [P, DM])
        k_shift = sb("k_shift", [P, DM])
        q_b, k_b, v_b = sb("q_b", [P, DM]), sb("k_b", [P, DM]), sb("v_b", [P, DM])
        q_e = sb("q_e", [P, DM])
        k_e = sb("k_e", [P, DM])
        k_n = sb("k_n", [P, 2, DM])
        qT = sb("qT", [P, G, TOK])
        kT = sb("kT", [P, G, TOK])
        q_heads = sb("q_heads", [P, 2, G, J, TOK])
        k_seqs = sb("k_seqs", [P, G, SEQS, TOK])
        v_seqs = sb("v_seqs", [P, 2, HEADS, SEQS, VW])
        att = sb("att", [P, G, J, TOK])
        st_masked = sb("st_masked", [P, G, J, VW])
        st_step = sb("st_step", [P, G, VW])
        st_run = sb("st_run", [P, G, VW])
        st_seqs = sb("st_seqs", [P, 2, G, SEQS, VW])
        den_rec = sb("den_rec", [P, 2, G // 2 * SEQS])
        a_n = sb("a_n", [P, SEQS, G, DH])
        ah = sb("ah", [P, J, P], F16)
        al = sb("al", [P, J, P], F16)
        o_sb = sb("o_sb", [P, 2, DM])
        q_ps = ps("q_ps", DM)
        k_ps = ps("k_ps", DM)
        vo_ps = ps("vo_ps", DM)
        t_ps = ps("t_ps", DM)
        s_ps = ps("s_ps", 2 * DM)
        a_ps = ps("a_ps", 2 * DM)
        s_state = s_ps[:, :].rearrange("p (n w) -> p n w", n=2)[:, :, 0:G // 2 * J * VW]
        a_view = a_ps[:, :].rearrange("p (n w) -> p n w", n=2)[:, :, 0:G // 2 * GW]
        aT_ps = a_ps[:, 0:DM]
        setup_banks = [q_ps, k_ps, vo_ps, t_ps]

        c_loaded, b_loaded, m_loaded = sem("c_loaded"), sem("b_loaded"), sem("m_loaded")
        w_loaded = [sem("w_loaded0"), sem("w_loaded1")]
        amax_ready, amax_shared = sem("amax_ready"), sem("amax_shared")
        chain = sem("chain")
        mult_ready, beta_exped = sem("mult_ready"), sem("beta_exped")
        wt_done, wh_ready, wl_ready = sem("wt_done"), sem("wh_ready"), sem("wl_ready")
        obias_ready, setup_done = sem("obias_ready"), sem("setup_done")
        x_loaded = [sem("x_loaded0"), sem("x_loaded1")]
        r_loaded = [sem("r_loaded0"), sem("r_loaded1")]
        stored = [sem("stored0"), sem("stored1")]
        stats_ready, mv_ready, rstd_ready = sem("stats_ready"), sem("mv_ready"), sem("rstd_ready")
        var_ready, half_ready, guess_ready = sem("var_ready"), sem("half_ready"), sem("guess_ready")
        newton_const = sem("newton_const")
        newton_steps = sem("newton_steps")
        xn_ready, xT_done, xh_ready, xl_ready = sem("xn_ready"), sem("xT_done"), sem("xh_ready"), sem("xl_ready")
        y_ready, yexp_ready, magic_ready = sem("y_ready"), sem("yexp_ready"), sem("magic_ready")
        ysum_ready, yround_ready, xq_ready = sem("ysum_ready"), sem("yround_ready"), sem("xq_ready")
        qb_ready, kb_ready, vb_ready = sem("qb_ready"), sem("kb_ready"), sem("vb_ready")
        q_done, k_done, v_done = sem("q_done"), sem("k_done"), sem("v_done")
        qmax_ready, qshift_ready, qe_ready = sem("qmax_ready"), sem("qshift_ready"), sem("qe_ready")
        kmax_ready, kshift_ready, ke_ready = sem("kmax_ready"), sem("kshift_ready"), sem("ke_ready")
        ksum_ready, krec_ready, kn_ready = sem("ksum_ready"), sem("krec_ready"), sem("kn_ready")
        qT_ready, kT_ready = sem("qT_ready"), sem("kT_ready")
        qheads_ready, kseqs_ready, vseqs_ready = sem("qheads_ready"), sem("kseqs_ready"), sem("vseqs_ready")
        scores_done, att_ready = sem("scores_done"), sem("att_ready")
        state_done, masked_ready, ststep_ready = sem("state_done"), sem("masked_ready"), sem("ststep_ready")
        strun_ready, stseqs_ready = sem("strun_ready"), sem("stseqs_ready")
        a_done, rec_ready, an_ready = sem("a_done"), sem("rec_ready"), sem("an_ready")
        aT_done, ah_ready, al_ready = sem("aT_done"), sem("ah_ready"), sem("al_ready")
        dve_waited, pe_waited = sem("dve_waited"), sem("pe_waited")
        f_done, o_done, o_ready = sem("f_done"), sem("o_done"), sem("o_ready")
        xres_ready = sem("xres_ready")

        block = ctx.enter_context(nc.Block())

        weights = [wq, wk, wv, wo, wf]
        turn = [MQ, MK, MV, MF, MO]
        loads = list(range(MATRICES)) + turn[:-1]
        wo_kept = att[:, :, :, :].rearrange("p g j s -> p (g j s)")\
            .rearrange("p (c n) -> p c n", c=KC)

        def heads(ap):
            return ap.rearrange("p (h d) -> p h d", d=DH)

        def per_head(ap):
            return ap[:, :, None].to_broadcast([P, HEADS, DH])

        @block.sync
        def _(sp):
            sp.dma_start(cst[:, :], const).then_inc(c_loaded, 16)
            for n, s in enumerate((beta, in_scale, w_scale)):
                sp.dma_start(scal[:, n:n + 1], s.rearrange("(a n) -> a n", a=1).to_broadcast([P, 1]))\
                    .then_inc(m_loaded, 16)
            for n, b in enumerate((bq, bk, bv, bo, bf)):
                sp.dma_start(bias[:, n, :], b.rearrange("(a n) -> a n", a=1).to_broadcast([P, DM]))\
                    .then_inc(b_loaded, 16)
            for r, m in enumerate(loads):
                if 2 <= r < MATRICES + 2:
                    sp.wait_ge(amax_ready, min(r - 1, MATRICES))
                if r >= MATRICES + 2:
                    sp.wait_ge(wt_done, KC * (r - 1 - MATRICES))
                sp.dma_start(w_nat[r % 2][:, :, :], weights[m].rearrange("(c p) d -> p c d", p=P))\
                    .then_inc(w_loaded[r % 2], 16)

            def load_x(t):
                if t.after(2):
                    sp.wait_ge(xn_ready, (t - 1).n)
                sp.dma_start(x_in[:, t.parity, :], x_t[t.n]).then_inc(x_loaded[t.parity], 16)

            def body(i):
                if (i + 1).exists():
                    load_x(i + 1)
                if i.exists():
                    if i.after(2):
                        sp.wait_ge(o_ready, (i - 1).n)
                    sp.dma_start(x_res[:, i.parity, :], x_t[i.n]).then_inc(r_loaded[i.parity], 16)

            iterations(sp, body)
            for n in range(2):
                sp.wait_ge(stored[n], 16 * (STEPS // 2))

        @block.gpsimd
        def _(pool):
            pool.wait_ge(amax_ready, MATRICES)
            nc.gpsimd.partition_all_reduce(amax_all[:, :], amax[:, :], P, bass.bass_isa.ReduceOp.max)\
                .then_inc(amax_shared, 1)
            nc.gpsimd.memset(three_halves[:, :], 1.5).then_inc(newton_const, 1)
            pool.wait_ge(newton_const, 1)
            pool.wait_ge(c_loaded, 16)

            pool.wait_ge(obias_ready, 1)

            def root(t):
                pool.wait_ge(guess_ready, (t + 1).n)
                if t.after(1):
                    pool.wait_ge(xn_ready, t.n)
                gp = nc.gpsimd
                r = guess[:, :]
                for n in range(NEWTON):
                    done = t.n * (4 * NEWTON - 1) + 4 * n
                    sq, half, plus, nxt = (newton[:, n, c:c + 1] for c in range(4))
                    if n:
                        pool.wait_ge(newton_steps, done)
                    gp.tensor_tensor(sq, r, r, ALU.mult).then_inc(newton_steps, 1)
                    pool.wait_ge(newton_steps, done + 1)
                    gp.tensor_tensor(half, sq, minus_half[:, :], ALU.mult).then_inc(newton_steps, 1)
                    pool.wait_ge(newton_steps, done + 2)
                    gp.tensor_tensor(plus, half, three_halves[:, :], ALU.add).then_inc(newton_steps, 1)
                    pool.wait_ge(newton_steps, done + 3)
                    gp.tensor_tensor(nxt, plus, r, ALU.mult)\
                        .then_inc(newton_steps if n < NEWTON - 1 else rstd_ready, 1)
                    r = nxt

            def body(i):
                if (i + 1).exists():
                    root(i + 1)
                if i.exists():
                    pool.wait_ge(r_loaded[i.parity], (i + 2).half * 16)
                    nc.gpsimd.tensor_tensor(x_res[:, i.parity, :], x_res[:, i.parity, :], bias[:, 3, :],
                                            ALU.add).then_inc(xres_ready, 1)
                    pool.wait_ge(krec_ready, (i + 1).n)
                    if i.after(2):
                        pool.wait_ge(state_done, (i - 1).n)
                    nc.gpsimd.tensor_tensor(heads(k_n[:, i.parity, :]), heads(k_e[:, :]),
                                            per_head(k_rec[:, :]), ALU.mult).then_inc(kn_ready, 1)
                    pool.wait_ge(kT_ready, (i + 1).n)
                    if i.after(1):
                        pool.wait_ge(scores_done, i.n * 4)
                    for c in range(4):
                        nc.gpsimd.tensor_tensor(
                            k_seqs[:, 4 * c:4 * c + 4, :, :],
                            kT[:, 4 * c:4 * c + 4, None, :].to_broadcast([P, 4, SEQS, TOK]),
                            seq_mask[:, None, :, None].to_broadcast([P, 4, SEQS, TOK]), ALU.mult)\
                            .then_inc(kseqs_ready, 1)
                t = i + 1
                if t.exists():
                    pool.wait_ge(y_ready, (t + 1).n)
                    pool.wait_ge(magic_ready, (t + 1).n)
                    nc.gpsimd.tensor_tensor(y_sum[:, :], y[:, :], y_magic[:, :], ALU.add)\
                        .then_inc(ysum_ready, 1)
                    pool.wait_ge(ysum_ready, (t + 1).n)
                    if t.after(1):
                        pool.wait_ge(xq_ready, t.n)
                    nc.gpsimd.tensor_tensor(y_round[:, :], y_sum[:, :], y_magic[:, :], ALU.subtract)\
                        .then_inc(yround_ready, 1)

            iterations(pool, body)

        @block.scalar
        def _(act):
            act.wait_ge(m_loaded, 48)
            nc.scalar.activation(exp_beta, scal[:, 0:1], ACT.Exp).then_inc(beta_exped, 1)
            act.wait_ge(mult_ready, 1)
            for n in range(MATRICES * KC):
                m, c = turn[n // KC], n % KC
                act.wait_ge(wt_done, n + 1)
                nc.scalar.activation(w_hi[:, m, c, :], setup_banks[n % 4][:, :], ACT.Copy,
                                     scale=w_mult[:, m:m + 1]).then_inc(wh_ready, 1)
            act.wait_ge(setup_done, 1)

            def body(i):
                if i.exists():
                    act.wait_ge(kshift_ready, (i + 1).n)
                    if i.after(1):
                        act.wait_ge(kn_ready, i.n)
                    nc.scalar.activation(k_e[:, :], k_shift[:, :], ACT.Exp, scale=k_exp_scale)\
                        .then_inc(ke_ready, 1)
                    act.wait_ge(qshift_ready, (i + 1).n)
                    if i.after(1):
                        act.wait_ge(qT_ready, i.n)
                    nc.scalar.activation(q_e[:, :], q_shift[:, :], ACT.Exp, scale=q_exp_scale)\
                        .then_inc(qe_ready, 1)
                    act.wait_ge(qT_ready, (i + 1).n)
                    for j in range(J):
                        last = nc.scalar.activation(q_heads[:, i.parity, :, j, :], qT[:, :, :],
                                                    ACT.Copy, scale=head_mask[:, j:j + 1])
                    last.then_inc(qheads_ready, 1)
                    act.wait_ge(vb_ready, (i + 1).n)
                    if i.after(2):
                        act.wait_ge(state_done, (i - 1).n)
                    for b in range(SEQS):
                        last = nc.scalar.activation(
                            v_seqs[:, i.parity, :, b, 0:DH],
                            v_b[:, :].rearrange("p (h d) -> p h d", d=DH),
                            ACT.Copy, scale=seq_mask[:, b:b + 1])
                    last.then_inc(vseqs_ready, 1)
                t = i + 1
                if t.exists():
                    act.wait_ge(xT_done, (t + 1).n)
                    if t.after(1):
                        act.wait_ge(v_done, t.n)
                    nc.scalar.activation(xh[:, :, :].rearrange("p c s -> p (c s)"), t_ps[:, :],
                                         ACT.Copy).then_inc(xh_ready, 1)
                    if t.after(1):
                        act.wait_ge(yround_ready, t.n)
                        act.wait_ge(magic_ready, t.n)
                    nc.scalar.activation(y[:, :], t_ps[:, :], ACT.Copy, scale=in_inv)\
                        .then_inc(y_ready, 1)
                t = i - 1
                if t.exists():
                    act.wait_ge(aT_done, (t + 1).n)
                    if t.after(1):
                        act.wait_ge(o_done, t.n)
                    nc.scalar.activation(ah[:, :, :].rearrange("p j s -> p (j s)"), aT_ps,
                                         ACT.Copy).then_inc(ah_ready, 1)
                    act.wait_ge(o_ready, (t + 1).n)
                    act.dma_start(out_t[t.n], o_sb[:, t.parity, :]).then_inc(stored[t.parity], 16)

            iterations(act, body)

        @block.vector
        def _(dve):
            links = [0]

            def link(instruction):
                instruction.then_inc(chain, 1)
                links[0] += 1
                dve.wait_ge(chain, links[0])

            v = nc.vector
            link(v.memset(st_run[:, :, :], 0.0))
            link(v.memset(st_seqs[:, 0, :, :, :], 0.0))
            dve.wait_ge(c_loaded, 16)
            for n in range(2):
                link(v.tensor_copy(v_seqs[:, n, :, :, DH],
                                   seq_mask[:, None, :].to_broadcast([P, HEADS, SEQS])))
            for r in range(MATRICES):
                dve.wait_ge(w_loaded[r % 2], 16 * (r // 2 + 1))
                if r == MO:
                    for oc in range(KC):
                        v.tensor_copy(wo_kept[:, oc, :].rearrange("p (j g d) -> p j g d", j=J, d=DH),
                                      w_nat[r % 2][:, oc, :].rearrange("p (g j d) -> p j g d", j=J, d=DH))
                v.tensor_reduce(amax[:, r:r + 1], w_nat[r % 2][:, :, :], AX.XY, ALU.max,
                                apply_absolute_value=True).then_inc(amax_ready, 1)
            dve.wait_ge(m_loaded, 48)
            link(v.tensor_tensor(both_scales, scal[:, 1:2], scal[:, 2:3], ALU.mult))
            link(v.tensor_scalar(tmp1, both_scales, -1.0, None, ALU.mult))
            link(v.tensor_tensor(abs_scales, both_scales, tmp1, ALU.max))
            dve.wait_ge(amax_shared, 1)
            link(v.tensor_tensor(amax_all[:, MF:MF + 1], amax_all[:, MF:MF + 1], abs_scales, ALU.mult))
            link(v.tensor_scalar(amax_all[:, :], amax_all[:, :], 1e-18, 1e18, ALU.max, ALU.min))
            link(v.tensor_scalar(w_top[:, :].bitcast(I32), amax_all[:, :].bitcast(I32), EXPONENT, None,
                                 ALU.bitwise_and))
            link(v.tensor_scalar(w_scale_dn[:, :], w_top[:, :], 2.0, None, ALU.mult))
            link(v.reciprocal(w_scale_up[:, :], w_scale_dn[:, :]))
            link(v.tensor_tensor(tmp1, w_scale_up[:, MO:MO + 1], w_scale_up[:, MV:MV + 1], ALU.mult))
            link(v.tensor_tensor(out_up, tmp1, w_scale_up[:, MF:MF + 1], ALU.min))
            link(v.reciprocal(out_dn, out_up))
            link(v.tensor_copy(w_mult[:, 0:MO], w_scale_up[:, 0:MO]))
            link(v.tensor_tensor(w_mult[:, MO:MO + 1], out_up, w_scale_dn[:, MV:MV + 1], ALU.mult))
            v.tensor_tensor(w_mult[:, MF:MF + 1], both_scales, out_up, ALU.mult).then_inc(mult_ready, 1)
            link(v.reciprocal(tmp2, scal[:, 1:2]))
            link(v.tensor_scalar(in_inv, tmp2, 1e30, -1e30, ALU.min, ALU.max))
            dve.wait_ge(beta_exped, 1)
            link(v.tensor_tensor(q_exp_scale, exp_beta, w_scale_dn[:, MQ:MQ + 1], ALU.mult))
            link(v.tensor_tensor(k_exp_scale, exp_beta, w_scale_dn[:, MK:MK + 1], ALU.mult))
            dve.wait_ge(b_loaded, 16 * 5)
            for m in (MQ, MK, MV):
                link(v.tensor_scalar(bias[:, m, :], bias[:, m, :], w_scale_up[:, m:m + 1], None, ALU.mult))
            v.tensor_tensor(bias[:, 3, :], bias[:, 3, :], bias[:, 4, :], ALU.add).then_inc(obias_ready, 1)
            dve.wait_ge(mult_ready, 1)
            for n in range(MATRICES * KC):
                m, c = turn[n // KC], n % KC
                dve.wait_ge(wh_ready, n + 1)
                v.scalar_tensor_tensor(w_lo[:, m, c, :], setup_banks[n % 4][:, :], w_mult[:, m:m + 1],
                                       w_hi[:, m, c, :], ALU.mult, ALU.subtract).then_inc(wl_ready, 1)
            dve.wait_ge(wl_ready, MATRICES * KC)
            v.tensor_copy(tmp1, tmp2).then_inc(setup_done, 1)

            def statistics(t):
                dve.wait_ge(x_loaded[t.parity], (t + 2).half * 16)
                v.bn_stats(stats[:, :], x_in[:, t.parity, :]).then_inc(stats_ready, 1)
                dve.wait_ge(stats_ready, (t + 1).n)
                if t.after(1):
                    dve.wait_ge(rstd_ready, t.n)
                dve.sem_inc(dve_waited, 1)
                v.bn_aggr(mv[:, t.parity, :], stats[:, :]).then_inc(mv_ready, 1)
                dve.wait_ge(mv_ready, (t + 1).n)
                v.tensor_scalar(var_e[:, :], mv[:, t.parity, 1:2], EPS, None, ALU.add).then_inc(var_ready, 1)
                v.tensor_scalar(minus_half[:, :], mv[:, t.parity, 1:2], EPS, -0.5, ALU.add, ALU.mult)
                dve.wait_ge(var_ready, (t + 1).n)
                v.tensor_scalar(shifted[:, :], var_e[:, :].bitcast(I32), 1, None,
                                ALU.logical_shift_right).then_inc(half_ready, 1)
                dve.wait_ge(half_ready, (t + 1).n)
                v.tensor_scalar(guess[:, :].bitcast(I32), shifted[:, :], -1, RSQRT_GUESS,
                                ALU.mult, ALU.add).then_inc(guess_ready, 1)

            def normalise(t):
                dve.wait_ge(rstd_ready, (t + 1).n)
                if t.after(1):
                    dve.wait_ge(xT_done, t.n)
                v.tensor_scalar(xn[:, :], x_in[:, t.parity, :], mv[:, t.parity, 0:1],
                                newton[:, NEWTON - 1, 3:4], ALU.subtract, ALU.mult).then_inc(xn_ready, 1)

            def shift(i, m, bank, done, added, added_ready, mx, mx_ready, sh, sh_ready, read):
                dve.wait_ge(done, (i + 1).n)
                v.tensor_tensor(added[:, :], bank[:, :], bias[:, m, :], ALU.add).then_inc(added_ready, 1)
                dve.wait_ge(added_ready, (i + 1).n)
                v.tensor_reduce(mx[:, :], heads(added[:, :]), AX.X, ALU.max).then_inc(mx_ready, 1)
                dve.wait_ge(mx_ready, (i + 1).n)
                if i.after(1):
                    dve.wait_ge(read, i.n)
                v.tensor_tensor(heads(sh[:, :]), heads(added[:, :]), per_head(mx[:, :]), ALU.subtract)\
                    .then_inc(sh_ready, 1)

            def state(i):
                dve.wait_ge(state_done, (i + 1).n)
                for n in range(2):
                    half = slice(n * G // 2, (n + 1) * G // 2)
                    last = v.tensor_tensor(
                        st_masked[:, half, :, :],
                        s_state[:, n, :].rearrange("p (g j w) -> p g j w", j=J, w=VW),
                        head_mask[:, None, :, None].to_broadcast([P, G // 2, J, VW]), ALU.mult)
                last.then_inc(masked_ready, 1)
                dve.wait_ge(masked_ready, (i + 1).n)
                v.tensor_reduce(st_step[:, :, :], st_masked[:, :, :, :].rearrange("p g j w -> p g w j"),
                                AX.X, ALU.add).then_inc(ststep_ready, 1)
                dve.wait_ge(ststep_ready, (i + 1).n)
                v.tensor_tensor(st_run[:, :, :], st_run[:, :, :], st_step[:, :, :], ALU.add)\
                    .then_inc(strun_ready, 1)
                dve.wait_ge(strun_ready, (i + 1).n)
                if i.after(1):
                    dve.wait_ge(a_done, i.n)
                v.tensor_tensor(st_seqs[:, (i + 1).parity, :, :, :],
                                st_run[:, :, None, :].to_broadcast([P, G, SEQS, VW]),
                                seq_mask[:, None, :, None].to_broadcast([P, G, SEQS, VW]), ALU.mult)\
                    .then_inc(stseqs_ready, 1)

            def mask_scores(i, c):
                dve.wait_ge(scores_done, i.n * 4 + c + 1)
                if c == 0 and i.after(1):
                    dve.wait_ge(a_done, i.n)
                v.tensor_tensor(att[:, 4 * c:4 * c + 4, :, :].rearrange("p g j s -> p (g j) s"),
                                s_ps[:, DM * (c % 2):DM * (c % 2 + 1)].rearrange("p (h s) -> p h s", s=TOK),
                                tri[:, None, :].to_broadcast([P, 4 * J, TOK]), ALU.mult)\
                    .then_inc(att_ready, 1)

            def body(i):
                t = i + 1
                if t.exists():
                    statistics(t)
                if i.exists():
                    shift(i, MK, k_ps, k_done, k_b, kb_ready, k_max, kmax_ready, k_shift, kshift_ready,
                          ke_ready)
                    shift(i, MQ, q_ps, q_done, q_b, qb_ready, q_max, qmax_ready, q_shift, qshift_ready,
                          qe_ready)
                    dve.wait_ge(ke_ready, (i + 1).n)
                    v.tensor_reduce(k_sum[:, :], heads(k_e[:, :]), AX.X, ALU.add).then_inc(ksum_ready, 1)
                    dve.wait_ge(ksum_ready, (i + 1).n)
                    v.reciprocal(k_rec[:, :], k_sum[:, :]).then_inc(krec_ready, 1)
                    dve.wait_ge(qe_ready, (i + 1).n)
                    if i.after(1):
                        dve.wait_ge(qheads_ready, i.n)
                    v.transpose(qT[:, :, :].rearrange("p g s -> p (g s)"), q_e[:, :]).then_inc(qT_ready, 1)
                    dve.wait_ge(v_done, (i + 1).n)
                    if i.after(1):
                        dve.wait_ge(vseqs_ready, i.n)
                    v.tensor_tensor(v_b[:, :], vo_ps[:, :], bias[:, MV, :], ALU.add).then_inc(vb_ready, 1)
                    dve.wait_ge(kn_ready, (i + 1).n)
                    if i.after(1):
                        dve.wait_ge(kseqs_ready, i.n * 4)
                    v.transpose(kT[:, :, :].rearrange("p g s -> p (g s)"), k_n[:, i.parity, :])\
                        .then_inc(kT_ready, 1)
                t = i + 1
                if t.exists():
                    normalise(t)
                t = i - 1
                if t.exists() and i.exists():
                    state(t)
                t = i - 1
                if t.exists():
                    dve.wait_ge(a_done, (t + 1).n)
                    for n in range(2):
                        a_n_ps = a_view[:, n, :].rearrange("p (m w) -> p m w", w=VW)
                        last = v.reciprocal(den_rec[:, n, :], a_n_ps[:, :, DH])
                    last.then_inc(rec_ready, 1)
                    dve.wait_ge(rec_ready, (t + 1).n)
                    if t.after(1):
                        dve.wait_ge(aT_done, t.n)
                    for n in range(2):
                        a_n_ps = a_view[:, n, :].rearrange("p (g b w) -> p g b w", b=SEQS, w=VW)
                        rec = den_rec[:, n, :].rearrange("p (g b) -> p g b", b=SEQS)
                        last = v.tensor_tensor(
                            a_n[:, :, n * G // 2:(n + 1) * G // 2, :].rearrange("p b g d -> p g b d"),
                            a_n_ps[:, :, :, 0:DH],
                            rec[:, :, :, None].to_broadcast([P, G // 2, SEQS, DH]), ALU.mult)
                    last.then_inc(an_ready, 1)
                if i.exists():
                    mask_scores(i, 0)
                    mask_scores(i, 1)
                t = i - 1
                if t.exists():
                    dve.wait_ge(ah_ready, (t + 1).n)
                    v.tensor_tensor(al[:, :, :].rearrange("p j s -> p (j s)"), aT_ps,
                                    ah[:, :, :].rearrange("p j s -> p (j s)"), ALU.subtract)\
                        .then_inc(al_ready, 1)
                if i.exists():
                    mask_scores(i, 2)
                    mask_scores(i, 3)
                t = i + 1
                if t.exists():
                    dve.wait_ge(xh_ready, (t + 1).n)
                    dve.wait_ge(y_ready, (t + 1).n)
                    v.tensor_tensor(xl[:, :, :].rearrange("p c s -> p (c s)"), t_ps[:, :],
                                    xh[:, :, :].rearrange("p c s -> p (c s)"), ALU.subtract)\
                        .then_inc(xl_ready, 1)
                t = i + 1
                if t.exists():
                    v.tensor_scalar(y_exp[:, :].bitcast(I32), y[:, :].bitcast(I32), EXPONENT, None,
                                    ALU.bitwise_and).then_inc(yexp_ready, 1)
                    dve.wait_ge(yexp_ready, (t + 1).n)
                    if t.after(1):
                        dve.wait_ge(yround_ready, t.n)
                    v.tensor_scalar(y_magic[:, :], y_exp[:, :], FP8_MIN_NORMAL, ROUND_TO_4_BITS,
                                    ALU.max, ALU.mult).then_inc(magic_ready, 1)
                t = i - 1
                if t.exists():
                    dve.wait_ge(o_done, (t + 1).n)
                    dve.wait_ge(xres_ready, (t + 1).n)
                    if t.after(2):
                        dve.wait_ge(stored[t.parity], t.half * 16)
                    v.scalar_tensor_tensor(o_sb[:, t.parity, :], vo_ps[:, :], out_dn,
                                           x_res[:, t.parity, :], ALU.mult, ALU.add).then_inc(o_ready, 1)
                t = i + 1
                if t.exists():
                    dve.wait_ge(yround_ready, (t + 1).n)
                    if t.after(2):
                        dve.wait_ge(f_done, (t - 1).n)
                    v.tensor_scalar(xq[:, t.parity, :, :].rearrange("p c s -> p (c s)"), y_round[:, :],
                                    FP8_MAX, -FP8_MAX, ALU.min, ALU.max).then_inc(xq_ready, 1)

            iterations(dve, body)

        @block.tensor
        def _(pe):
            mm = nc.tensor.matmul
            pe.wait_ge(c_loaded, 16)
            for k, m in enumerate(turn):
                r = MATRICES + k
                if m == MO:
                    pe.wait_ge(amax_ready, MATRICES)
                else:
                    pe.wait_ge(w_loaded[r % 2], 16 * (r // 2 + 1))
                for c in range(KC):
                    n = k * KC + c
                    if n >= 4:
                        pe.wait_ge(wl_ready, n - 3)
                    for oc in range(KC):
                        src = (wo_kept if m == MO else w_nat[r % 2])[:, oc, c * P:(c + 1) * P]
                        last = nc.tensor.transpose(setup_banks[n % 4][:, oc * P:(oc + 1) * P], src, ident)
                    last.then_inc(wt_done, 1)
            pe.wait_ge(setup_done, 1)

            def a_col(g):
                return DM * (g // (G // 2)) + GW * (g % (G // 2))

            def project(bank, m):
                for c in range(KC):
                    mm(bank[:, :], xh[:, c, :], w_hi[:, m, c, :], start=(c == 0), stop=False)
                    mm(bank[:, :], xh[:, c, :], w_lo[:, m, c, :], start=False, stop=False)
                    last = mm(bank[:, :], xl[:, c, :], w_hi[:, m, c, :], start=False, stop=(c == KC - 1))
                return last

            def scores(i, c):
                pe.wait_ge(kseqs_ready, i.n * 4 + c + 1)
                if c < 2:
                    if i.after(1):
                        pe.wait_ge(masked_ready, i.n)
                else:
                    pe.wait_ge(att_ready, i.n * 4 + c - 1)
                for gg in range(4):
                    g = 4 * c + gg
                    last = mm(s_ps[:, DM * (c % 2) + P * gg:DM * (c % 2) + P * (gg + 1)],
                              k_seqs[:, g, :, :], q_heads[:, i.parity, g, :, :], start=True, stop=True)
                last.then_inc(scores_done, 1)

            def body(i):
                if i.exists():
                    pe.wait_ge(xh_ready, (i + 1).n)
                    pe.wait_ge(xl_ready, (i + 1).n)
                    if i.after(1):
                        pe.wait_ge(kb_ready, i.n)
                    project(k_ps, MK).then_inc(k_done, 1)
                t = i - 1
                if t.exists() and i.exists():
                    pe.wait_ge(kn_ready, (t + 1).n)
                    pe.wait_ge(vseqs_ready, (t + 1).n)
                    pe.wait_ge(att_ready, (t + 1).n * 4)
                    pe.sem_inc(pe_waited, 1)
                    for g in range(G):
                        col = DM * (g // (G // 2)) + J * VW * (g % (G // 2))
                        for b in range(SEQS):
                            rows = slice(TOK * b, TOK * (b + 1))
                            last = mm(s_ps[rows, col:col + J * VW], k_n[rows, t.parity, TOK * g:TOK * (g + 1)],
                                      v_seqs[rows, t.parity, J * g:J * (g + 1), b, :], start=True, stop=True)
                    last.then_inc(state_done, 1)
                if i.exists():
                    if i.after(1):
                        pe.wait_ge(qb_ready, i.n)
                    project(q_ps, MQ).then_inc(q_done, 1)
                    if i.after(2):
                        pe.wait_ge(o_ready, (i - 1).n)
                    project(vo_ps, MV).then_inc(v_done, 1)
                t = i - 1
                if t.exists():
                    if t.after(1):
                        pe.wait_ge(stseqs_ready, t.n)
                        pe.wait_ge(al_ready, t.n)
                    pe.wait_ge(qheads_ready, (t + 1).n)
                    for g in range(G):
                        for j in range(J):
                            mm(a_ps[TOK * j:TOK * (j + 1), a_col(g):a_col(g) + GW],
                               q_heads[:, t.parity, g, j, :], st_seqs[:, t.parity, g, :, :],
                               start=(g % (G // 2) == 0), stop=False, skip_group_check=True)
                    pe.wait_ge(att_ready, (t + 1).n * 4)
                    pe.wait_ge(vseqs_ready, (t + 1).n)
                    for g in range(G):
                        for j in range(J):
                            last = mm(a_ps[TOK * j:TOK * (j + 1), a_col(g):a_col(g) + GW], att[:, g, j, :],
                                      v_seqs[:, t.parity, J * g + j, :, :], start=False, stop=True,
                                      skip_group_check=True)
                    last.then_inc(a_done, 1)
                    pe.wait_ge(xq_ready, (t + 1).n)
                    if i.exists():
                        pe.wait_ge(vb_ready, (i + 1).n)
                    else:
                        pe.wait_ge(o_ready, t.n)
                    for c in range(KC):
                        mm(vo_ps[:, :], xq[:, t.parity, c, :], w_hi[:, MF, c, :], start=(c == 0), stop=False)
                        last = mm(vo_ps[:, :], xq[:, t.parity, c, :], w_lo[:, MF, c, :], start=False,
                                  stop=False)
                    last.then_inc(f_done, 1)
                t = i + 1
                if t.exists():
                    pe.wait_ge(xn_ready, (t + 1).n)
                    if t.after(1):
                        pe.wait_ge(xl_ready, t.n)
                    for c in range(KC):
                        last = nc.tensor.transpose(t_ps[:, P * c:P * (c + 1)], xn[:, P * c:P * (c + 1)], ident)
                    last.then_inc(xT_done, 1)
                if i.exists():
                    pe.wait_ge(qheads_ready, (i + 1).n)
                    scores(i, 0)
                    scores(i, 1)
                t = i - 1
                if t.exists():
                    pe.wait_ge(an_ready, (t + 1).n)
                    for b in range(SEQS):
                        last = nc.tensor.transpose(
                            aT_ps.rearrange("p (j b s) -> p b j s", b=SEQS, s=TOK)[:, b],
                            a_n[:, b, :, :].rearrange("p g d -> p (g d)"), ident)
                    last.then_inc(aT_done, 1)
                if i.exists():
                    scores(i, 2)
                    scores(i, 3)
                if t.exists():
                    pe.wait_ge(ah_ready, (t + 1).n)
                    pe.wait_ge(al_ready, (t + 1).n)
                    for j in range(J):
                        mm(vo_ps[:, :], ah[:, j, :], w_hi[:, MO, j, :], start=False, stop=False)
                        mm(vo_ps[:, :], ah[:, j, :], w_lo[:, MO, j, :], start=False, stop=False)
                        last = mm(vo_ps[:, :], al[:, j, :], w_hi[:, MO, j, :], start=False, stop=(j == J - 1))
                    last.then_inc(o_done, 1)

            iterations(pe, body)


_INS = ["L0_attn_x", "L0_attn_Wq", "L0_attn_bq", "L0_attn_Wk", "L0_attn_bk", "L0_attn_Wv", "L0_attn_bv",
        "L0_attn_Wo", "L0_attn_bo", "L0_attn_beta", "L0_ffn_weight_fp8", "L0_ffn_bias",
        "L0_ffn_input_scale", "L0_ffn_weight_scale"]


def constants():
    c = np.zeros((P, C_ALL), np.float32)
    p = np.arange(P)
    c[:, C_ID:C_ID + P] = np.eye(P)
    c[:, C_HEAD:C_HEAD + J] = (p[:, None] % TOK) // DH == np.arange(J)
    c[:, C_SEQ:C_SEQ + SEQS] = p[:, None] // TOK == np.arange(SEQS)
    c[:, C_TRI:C_TRI + TOK] = p[:, None] % TOK <= np.arange(TOK)
    return c


def kernel(**inputs):
    import concourse.bacc as bacc
    from concourse.bass_utils import run_bass_kernel_spmd

    nc = bacc.Bacc("TRN2", target_bir_lowering=False, num_devices=1)
    arrays = {name: np.ascontiguousarray(inputs[name]) for name in _INS}
    arrays["const"] = constants()
    args = [nc.dram_tensor(name, a.shape, F32, kind="ExternalInput").ap() for name, a in arrays.items()]
    out = nc.dram_tensor("out", (SEQS, LEN, DM), F32, kind="ExternalOutput").ap()
    build(nc, *args, out)
    r = run_bass_kernel_spmd(nc, [arrays], core_ids=[0])
    return r.results[0]["out"]
```

```python
from contextlib import ExitStack

import numpy as np
import concourse.bass as bass
import concourse.mybir as mybir

F32 = mybir.dt.float32
F16 = mybir.dt.float16
BF16 = mybir.dt.bfloat16
I32 = mybir.dt.int32
ALU = mybir.AluOpType
ACT = mybir.ActivationFunctionType
AX = mybir.AxisListType

P = 128
SEQS = 4
TOK = P // SEQS
LEN = 2048
DM = 512
HEADS = 64
DH = DM // HEADS
J = 4
G = HEADS // J
KC = DM // P
STEPS = LEN // TOK
PEELED = 3
VW = DH + 1
GW = SEQS * VW
EPS = 1e-5
FP8_MAX = 448.0
FP8_MIN_NORMAL = 2.0 ** -6
ROUND_TO_4_BITS = 1.5 * 2.0 ** 20
EXPONENT = 0x7F800000
RSQRT_GUESS = 0x5F3759DF
NEWTON = 3
MATRICES = 5
MQ, MK, MV, MO, MF = range(MATRICES)
C_ID = 0
C_HEAD = C_ID + P
C_SEQ = C_HEAD + J
C_TRI = C_SEQ + SEQS
C_ALL = C_TRI + TOK


class Step:

    def __init__(self, k, off):
        self.k, self.off = k, off

    def __add__(self, n):
        return Step(self.k, self.off + n)

    def __sub__(self, n):
        return self + (-n)

    @property
    def n(self):
        return self.k * 2 + self.off

    @property
    def parity(self):
        return self.off % 2

    @property
    def half(self):
        return self.k + self.off // 2

    def exists(self):
        return not isinstance(self.k, int) or 0 <= self.off < STEPS

    def after(self, n):
        return not isinstance(self.k, int) or self.off >= n


def iterations(eng, body, first=0):
    for i in range(first, PEELED):
        body(Step(0, i))
    with eng.Fori(0, (STEPS - 1 - PEELED) // 2) as k:
        body(Step(k, PEELED))
        body(Step(k, PEELED + 1))
    body(Step(0, STEPS - 1))
    body(Step(0, STEPS))


def build(nc, x, wq, bq, wk, bk, wv, bv, wo, bo, beta, wf, bf, in_scale, w_scale, const, out):
    x_t = x.rearrange("b (t s) d -> t b s d", s=TOK)
    out_t = out.rearrange("b (t s) d -> t b s d", s=TOK)

    with ExitStack() as ctx:
        def sb(name, shape, dt=F32):
            return ctx.enter_context(nc.sbuf_tensor(name, shape, dt))

        def ps(name, cols):
            return ctx.enter_context(nc.psum_tensor(name, [P, cols], F32))

        def sem(name):
            return ctx.enter_context(nc.semaphore(name))

        cst = sb("cst", [P, C_ALL])
        ident = cst[:, C_ID:C_ID + P]
        head_mask = cst[:, C_HEAD:C_HEAD + J]
        seq_mask = cst[:, C_SEQ:C_SEQ + SEQS]
        tri = cst[:, C_TRI:C_TRI + TOK]
        w_hi = sb("w_hi", [P, MATRICES, KC, DM], F16)
        w_lo = sb("w_lo", [P, MATRICES, KC, DM], F16)
        w_nat = [sb(f"w_nat{n}", [P, KC, DM]) for n in range(2)]
        bias = sb("bias", [P, 5, DM])
        scal = sb("scal", [P, 3])
        amax = sb("amax", [P, MATRICES])
        amax_all = sb("amax_all", [P, MATRICES])
        w_top = sb("w_top", [P, MATRICES])
        w_scale_up = sb("w_scale_up", [P, MATRICES])
        w_scale_dn = sb("w_scale_dn", [P, MATRICES])
        w_mult = sb("w_mult", [P, MATRICES])
        both_scales, exp_beta = sb("both_scales", [P, 1]), sb("exp_beta", [P, 1])
        q_exp_scale, k_exp_scale = sb("q_exp_scale", [P, 1]), sb("k_exp_scale", [P, 1])
        out_up, out_dn = sb("out_up", [P, 1]), sb("out_dn", [P, 1])
        in_rec, in_inv = sb("in_rec", [P, 1]), sb("in_inv", [P, 1])
        neg_scales, abs_scales = sb("neg_scales", [P, 1]), sb("abs_scales", [P, 1])
        up_product = sb("up_product", [P, 1])
        lo_abs = sb("lo_abs", [P, KC * DM], F16)
        lo_sum, lo_total = sb("lo_sum", [P, 1]), sb("lo_total", [P, 1])
        x_in = sb("x_in", [P, 2, DM])
        x_res = sb("x_res", [P, 2, DM])
        stats = sb("stats", [P, 6])
        mv = sb("mv", [P, 2, 2])
        var_e = sb("var_e", [P, 1])
        shifted = sb("shifted", [P, 1], I32)
        minus_half = sb("minus_half", [P, 1])
        three_halves = sb("three_halves", [P, 1])
        guess = sb("guess", [P, 1])
        newton = sb("newton", [P, NEWTON, 4])
        xn = sb("xn", [P, DM])
        xh = sb("xh", [P, KC, P], F16)
        xl = sb("xl", [P, KC, P], F16)
        y = sb("y", [P, DM])
        y_exp = sb("y_exp", [P, DM])
        y_magic = sb("y_magic", [P, DM])
        y_sum = sb("y_sum", [P, DM])
        y_round = sb("y_round", [P, DM])
        xq = sb("xq", [P, 2, KC, P], F16)
        q_max = sb("q_max", [P, HEADS])
        k_max = sb("k_max", [P, HEADS])
        k_sum = sb("k_sum", [P, HEADS])
        k_rec = sb("k_rec", [P, HEADS])
        q_shift = sb("q_shift", [P, DM])
        k_shift = sb("k_shift", [P, DM])
        q_b, k_b, v_b = sb("q_b", [P, DM]), sb("k_b", [P, DM]), sb("v_b", [P, DM])
        q_e = sb("q_e", [P, DM])
        k_e = sb("k_e", [P, DM])
        k_n = sb("k_n", [P, 2, DM])
        qT = sb("qT", [P, G, TOK])
        kT = sb("kT", [P, G, TOK])
        q_heads = sb("q_heads", [P, 2, G, J, TOK])
        k_seqs = sb("k_seqs", [P, G, SEQS, TOK])
        v_seqs = sb("v_seqs", [P, 2, HEADS, SEQS, VW])
        att = sb("att", [P, G, J, TOK])
        st_masked = sb("st_masked", [P, G, J, VW])
        st_step = sb("st_step", [P, G, VW])
        st_run = sb("st_run", [P, G, VW])
        st_seqs = sb("st_seqs", [P, 2, G, SEQS, VW])
        den_rec = sb("den_rec", [P, 2, G // 2 * SEQS])
        a_n = sb("a_n", [P, SEQS, G, DH])
        ah = sb("ah", [P, J, P], F16)
        al = sb("al", [P, J, P], F16)
        o_sb = sb("o_sb", [P, 2, DM])
        q_ps = ps("q_ps", DM)
        k_ps = ps("k_ps", DM)
        vo_ps = ps("vo_ps", DM)
        t_ps = ps("t_ps", DM)
        s_ps = ps("s_ps", 2 * DM)
        a_ps = ps("a_ps", 2 * DM)
        s_state = s_ps[:, :].rearrange("p (n w) -> p n w", n=2)[:, :, 0:G // 2 * J * VW]
        a_view = a_ps[:, :].rearrange("p (n w) -> p n w", n=2)[:, :, 0:G // 2 * GW]
        aT_ps = a_ps[:, 0:DM]
        setup_banks = [b[:, n * DM:(n + 1) * DM] for b, n in
                       ((q_ps, 0), (k_ps, 0), (vo_ps, 0), (s_ps, 0), (s_ps, 1), (a_ps, 0), (a_ps, 1))]

        c_loaded, b_loaded, m_loaded = sem("c_loaded"), sem("b_loaded"), sem("m_loaded")
        w_loaded = [sem(f"w_loaded{n}") for n in range(MATRICES)]
        amax_ready, amax_shared = sem("amax_ready"), sem("amax_shared")
        chain = sem("chain")
        mult_ready, beta_exped, in_inv_ready = sem("mult_ready"), sem("beta_exped"), sem("in_inv_ready")
        wo_ordered, lo_summed, lo_shared = sem("wo_ordered"), sem("lo_summed"), sem("lo_shared")
        wt_done, wh_ready, wl_ready = sem("wt_done"), sem("wh_ready"), sem("wl_ready")
        obias_ready = sem("obias_ready")
        x_loaded = [sem("x_loaded0"), sem("x_loaded1")]
        r_loaded = [sem("r_loaded0"), sem("r_loaded1")]
        stored = [sem("stored0"), sem("stored1")]
        stats_ready, mv_ready, rstd_ready = sem("stats_ready"), sem("mv_ready"), sem("rstd_ready")
        var_ready, half_ready, guess_ready = sem("var_ready"), sem("half_ready"), sem("guess_ready")
        newton_const = sem("newton_const")
        newton_steps = sem("newton_steps")
        xn_ready, xT_done, xh_ready, xl_ready = sem("xn_ready"), sem("xT_done"), sem("xh_ready"), sem("xl_ready")
        y_ready, yexp_ready, magic_ready = sem("y_ready"), sem("yexp_ready"), sem("magic_ready")
        ysum_ready, yround_ready, xq_ready = sem("ysum_ready"), sem("yround_ready"), sem("xq_ready")
        qb_ready, kb_ready, vb_ready = sem("qb_ready"), sem("kb_ready"), sem("vb_ready")
        q_done, k_done, v_done = sem("q_done"), sem("k_done"), sem("v_done")
        qmax_ready, qshift_ready, qe_ready = sem("qmax_ready"), sem("qshift_ready"), sem("qe_ready")
        kmax_ready, kshift_ready, ke_ready = sem("kmax_ready"), sem("kshift_ready"), sem("ke_ready")
        ksum_ready, krec_ready, kn_ready = sem("ksum_ready"), sem("krec_ready"), sem("kn_ready")
        qT_ready, kT_ready = sem("qT_ready"), sem("kT_ready")
        qheads_ready, kseqs_ready, vseqs_ready = sem("qheads_ready"), sem("kseqs_ready"), sem("vseqs_ready")
        scores_done, att_ready = sem("scores_done"), sem("att_ready")
        state_done, masked_ready, ststep_ready = sem("state_done"), sem("masked_ready"), sem("ststep_ready")
        strun_ready, stseqs_ready = sem("strun_ready"), sem("stseqs_ready")
        a_done, rec_ready, an_ready = sem("a_done"), sem("rec_ready"), sem("an_ready")
        aT_done, ah_ready, al_ready = sem("aT_done"), sem("ah_ready"), sem("al_ready")
        dve_waited, pe_waited = sem("dve_waited"), sem("pe_waited")
        f_done, o_done, o_ready = sem("f_done"), sem("o_done"), sem("o_ready")
        xres_ready = sem("xres_ready")

        block = ctx.enter_context(nc.Block())

        weights = [wq, wk, wv, wo, wf]
        turn = [MK, MQ, MV, MO, MF]

        def flat(ap):
            return ap.rearrange("p g j s -> p (g j s)").rearrange("p (c n) -> p c n", c=KC)

        staged = {MK: w_nat[0][:, :, :], MQ: w_nat[1][:, :, :], MV: flat(q_heads[:, 0]),
                  MO: flat(k_seqs[:, :, :, :]), MF: flat(q_heads[:, 1])}
        wo_kept = flat(att[:, :, :, :])
        chunks = MATRICES * KC
        attention_chunks = 3 * KC

        def heads(ap):
            return ap.rearrange("p (h d) -> p h d", d=DH)

        def per_head(ap):
            return ap[:, :, None].to_broadcast([P, HEADS, DH])

        @block.sync
        def _(sp):
            def load_x(t):
                if t.after(2):
                    sp.wait_ge(xn_ready, (t - 1).n)
                sp.dma_start(x_in[:, t.parity, :], x_t[t.n]).then_inc(x_loaded[t.parity], 16)

            def body(i):
                if (i + 1).exists():
                    load_x(i + 1)
                if i.exists():
                    if i.after(2):
                        sp.wait_ge(o_ready, (i - 1).n)
                    sp.dma_start(x_res[:, i.parity, :], x_t[i.n]).then_inc(r_loaded[i.parity], 16)

            body(Step(0, -1))
            for m in turn:
                sp.dma_start(staged[m], weights[m].rearrange("(c p) d -> p c d", p=P))\
                    .then_inc(w_loaded[m], 16)
            iterations(sp, body)
            for n in range(2):
                sp.wait_ge(stored[n], 16 * (STEPS // 2))

        @block.gpsimd
        def _(pool):
            nc.gpsimd.memset(three_halves[:, :], 1.5).then_inc(newton_const, 1)
            pool.wait_ge(newton_const, 1)

            def root(t):
                pool.wait_ge(guess_ready, (t + 1).n)
                if t.after(1):
                    pool.wait_ge(xn_ready, t.n)
                gp = nc.gpsimd
                r = guess[:, :]
                for n in range(NEWTON):
                    done = t.n * (4 * NEWTON - 1) + 4 * n
                    sq, half, plus, nxt = (newton[:, n, c:c + 1] for c in range(4))
                    if n:
                        pool.wait_ge(newton_steps, done)
                    gp.tensor_tensor(sq, r, r, ALU.mult).then_inc(newton_steps, 1)
                    pool.wait_ge(newton_steps, done + 1)
                    gp.tensor_tensor(half, sq, minus_half[:, :], ALU.mult).then_inc(newton_steps, 1)
                    pool.wait_ge(newton_steps, done + 2)
                    gp.tensor_tensor(plus, half, three_halves[:, :], ALU.add).then_inc(newton_steps, 1)
                    pool.wait_ge(newton_steps, done + 3)
                    gp.tensor_tensor(nxt, plus, r, ALU.mult)\
                        .then_inc(newton_steps if n < NEWTON - 1 else rstd_ready, 1)
                    r = nxt

            def body(i):
                if (i + 1).exists():
                    root(i + 1)
                if i.exists():
                    pool.wait_ge(r_loaded[i.parity], (i + 2).half * 16)
                    nc.gpsimd.tensor_tensor(x_res[:, i.parity, :], x_res[:, i.parity, :], bias[:, 3, :],
                                            ALU.add).then_inc(xres_ready, 1)
                    pool.wait_ge(krec_ready, (i + 1).n)
                    if i.after(2):
                        pool.wait_ge(state_done, (i - 1).n)
                    nc.gpsimd.tensor_tensor(heads(k_n[:, i.parity, :]), heads(k_e[:, :]),
                                            per_head(k_rec[:, :]), ALU.mult).then_inc(kn_ready, 1)
                    pool.wait_ge(kT_ready, (i + 1).n)
                    if i.after(1):
                        pool.wait_ge(scores_done, i.n * 4)
                    for c in range(4):
                        nc.gpsimd.tensor_tensor(
                            k_seqs[:, 4 * c:4 * c + 4, :, :],
                            kT[:, 4 * c:4 * c + 4, None, :].to_broadcast([P, 4, SEQS, TOK]),
                            seq_mask[:, None, :, None].to_broadcast([P, 4, SEQS, TOK]), ALU.mult)\
                            .then_inc(kseqs_ready, 1)
                t = i + 1
                if t.exists():
                    pool.wait_ge(y_ready, (t + 1).n)
                    pool.wait_ge(magic_ready, (t + 1).n)
                    nc.gpsimd.tensor_tensor(y_sum[:, :], y[:, :], y_magic[:, :], ALU.add)\
                        .then_inc(ysum_ready, 1)
                    pool.wait_ge(ysum_ready, (t + 1).n)
                    if t.after(1):
                        pool.wait_ge(xq_ready, t.n)
                    nc.gpsimd.tensor_tensor(y_round[:, :], y_sum[:, :], y_magic[:, :], ALU.subtract)\
                        .then_inc(yround_ready, 1)

            body(Step(0, -1))
            pool.wait_ge(amax_ready, 3)
            nc.gpsimd.partition_all_reduce(amax_all[:, 0:MO], amax[:, 0:MO], P, bass.bass_isa.ReduceOp.max)\
                .then_inc(amax_shared, 1)
            pool.wait_ge(amax_ready, MATRICES)
            nc.gpsimd.partition_all_reduce(amax_all[:, MO:], amax[:, MO:], P, bass.bass_isa.ReduceOp.max)\
                .then_inc(amax_shared, 1)
            pool.wait_ge(b_loaded, 16 * 5)
            nc.gpsimd.tensor_tensor(bias[:, 3, :], bias[:, 3, :], bias[:, 4, :], ALU.add)\
                .then_inc(obias_ready, 1)
            pool.wait_ge(lo_summed, 1)
            nc.gpsimd.partition_all_reduce(lo_total[:, :], lo_sum[:, :], P, bass.bass_isa.ReduceOp.max)\
                .then_inc(lo_shared, 1)
            pool.wait_ge(obias_ready, 1)
            pool.wait_ge(wt_done, chunks)
            iterations(pool, body)

        @block.scalar
        def _(act):
            act.dma_start(cst[:, :], const).then_inc(c_loaded, 16)
            for n, s in enumerate((beta, in_scale, w_scale)):
                act.dma_start(scal[:, n:n + 1], s.rearrange("(a n) -> a n", a=1).to_broadcast([P, 1]))\
                    .then_inc(m_loaded, 16)
            for n, b in enumerate((bq, bk, bv, bo, bf)):
                act.dma_start(bias[:, n, :], b.rearrange("(a n) -> a n", a=1).to_broadcast([P, DM]))\
                    .then_inc(b_loaded, 16)
            act.wait_ge(m_loaded, 48)
            nc.scalar.activation(exp_beta[:, :], scal[:, 0:1], ACT.Exp).then_inc(beta_exped, 1)
            act.wait_ge(in_inv_ready, 1)

            def body(i):
                if i.exists():
                    act.wait_ge(kshift_ready, (i + 1).n)
                    if i.after(1):
                        act.wait_ge(kn_ready, i.n)
                    nc.scalar.activation(k_e[:, :], k_shift[:, :], ACT.Exp, scale=k_exp_scale[:, :])\
                        .then_inc(ke_ready, 1)
                    act.wait_ge(qshift_ready, (i + 1).n)
                    if i.after(1):
                        act.wait_ge(qT_ready, i.n)
                    nc.scalar.activation(q_e[:, :], q_shift[:, :], ACT.Exp, scale=q_exp_scale[:, :])\
                        .then_inc(qe_ready, 1)
                    act.wait_ge(qT_ready, (i + 1).n)
                    for j in range(J):
                        last = nc.scalar.activation(q_heads[:, i.parity, :, j, :], qT[:, :, :],
                                                    ACT.Copy, scale=head_mask[:, j:j + 1])
                    last.then_inc(qheads_ready, 1)
                    act.wait_ge(vb_ready, (i + 1).n)
                    if i.after(2):
                        act.wait_ge(state_done, (i - 1).n)
                    for b in range(SEQS):
                        last = nc.scalar.activation(
                            v_seqs[:, i.parity, :, b, 0:DH],
                            v_b[:, :].rearrange("p (h d) -> p h d", d=DH),
                            ACT.Copy, scale=seq_mask[:, b:b + 1])
                    last.then_inc(vseqs_ready, 1)
                t = i + 1
                if t.exists():
                    act.wait_ge(xT_done, (t + 1).n)
                    if t.after(1):
                        act.wait_ge(v_done, t.n)
                    nc.scalar.activation(xh[:, :, :].rearrange("p c s -> p (c s)"), t_ps[:, :],
                                         ACT.Copy).then_inc(xh_ready, 1)
                    if t.after(1):
                        act.wait_ge(yround_ready, t.n)
                        act.wait_ge(magic_ready, t.n)
                    nc.scalar.activation(y[:, :], t_ps[:, :], ACT.Copy, scale=in_inv[:, :])\
                        .then_inc(y_ready, 1)
                t = i - 1
                if t.exists():
                    act.wait_ge(aT_done, (t + 1).n)
                    if t.after(1):
                        act.wait_ge(o_done, t.n)
                    nc.scalar.activation(ah[:, :, :].rearrange("p j s -> p (j s)"), aT_ps,
                                         ACT.Copy).then_inc(ah_ready, 1)
                    act.wait_ge(o_ready, (t + 1).n)
                    act.dma_start(out_t[t.n], o_sb[:, t.parity, :]).then_inc(stored[t.parity], 16)

            body(Step(0, -1))

            def high_parts(m):
                for c in range(KC):
                    n = turn.index(m) * KC + c
                    act.wait_ge(wt_done, n + 1)
                    nc.scalar.activation(w_hi[:, m, c, :], setup_banks[n % len(setup_banks)], ACT.Copy,
                                         scale=w_mult[:, m:m + 1]).then_inc(wh_ready, 1)

            act.wait_ge(mult_ready, 1)
            high_parts(MK)
            act.wait_ge(w_loaded[MO], 16)
            for oc in range(KC):
                last = nc.scalar.activation(wo_kept[:, oc, :].rearrange("p (j g d) -> p j g d", j=J, d=DH),
                                            staged[MO][:, oc, :].rearrange("p (g j d) -> p j g d", j=J, d=DH),
                                            ACT.Copy)
            last.then_inc(wo_ordered, 1)
            high_parts(MQ)
            high_parts(MV)
            act.wait_ge(mult_ready, 2)
            high_parts(MO)
            high_parts(MF)
            act.wait_ge(wl_ready, chunks)
            nc.scalar.activation(lo_abs[:, :], w_lo[:, MF, :, :].rearrange("p c d -> p (c d)"), ACT.Abs,
                                 accum_out=lo_sum[:, :]).then_inc(lo_summed, 1)
            iterations(act, body)

        @block.vector
        def _(dve):
            links = [0]

            def link(instruction):
                instruction.then_inc(chain, 1)
                links[0] += 1
                dve.wait_ge(chain, links[0])

            v = nc.vector
            link(v.memset(st_run[:, :, :], 0.0))
            link(v.memset(st_seqs[:, 0, :, :, :], 0.0))
            dve.wait_ge(c_loaded, 16)
            for n in range(2):
                link(v.tensor_copy(v_seqs[:, n, :, :, DH],
                                   seq_mask[:, None, :].to_broadcast([P, HEADS, SEQS])))
            def statistics(t):
                dve.wait_ge(x_loaded[t.parity], (t + 2).half * 16)
                v.bn_stats(stats[:, :], x_in[:, t.parity, :]).then_inc(stats_ready, 1)
                dve.wait_ge(stats_ready, (t + 1).n)
                if t.after(1):
                    dve.wait_ge(rstd_ready, t.n)
                dve.sem_inc(dve_waited, 1)
                v.bn_aggr(mv[:, t.parity, :], stats[:, :]).then_inc(mv_ready, 1)
                dve.wait_ge(mv_ready, (t + 1).n)
                v.tensor_scalar(var_e[:, :], mv[:, t.parity, 1:2], EPS, None, ALU.add).then_inc(var_ready, 1)
                v.tensor_scalar(minus_half[:, :], mv[:, t.parity, 1:2], EPS, -0.5, ALU.add, ALU.mult)
                dve.wait_ge(var_ready, (t + 1).n)
                v.tensor_scalar(shifted[:, :], var_e[:, :].bitcast(I32), 1, None,
                                ALU.logical_shift_right).then_inc(half_ready, 1)
                dve.wait_ge(half_ready, (t + 1).n)
                v.tensor_scalar(guess[:, :].bitcast(I32), shifted[:, :], -1, RSQRT_GUESS,
                                ALU.mult, ALU.add).then_inc(guess_ready, 1)

            def normalise(t):
                dve.wait_ge(rstd_ready, (t + 1).n)
                if t.after(1):
                    dve.wait_ge(xT_done, t.n)
                v.tensor_scalar(xn[:, :], x_in[:, t.parity, :], mv[:, t.parity, 0:1],
                                newton[:, NEWTON - 1, 3:4], ALU.subtract, ALU.mult).then_inc(xn_ready, 1)

            def low_input(t):
                dve.wait_ge(xh_ready, (t + 1).n)
                dve.wait_ge(y_ready, (t + 1).n)
                v.tensor_tensor(xl[:, :, :].rearrange("p c s -> p (c s)"), t_ps[:, :],
                                xh[:, :, :].rearrange("p c s -> p (c s)"), ALU.subtract)\
                    .then_inc(xl_ready, 1)

            def magic(t):
                v.tensor_scalar(y_exp[:, :].bitcast(I32), y[:, :].bitcast(I32), EXPONENT, None,
                                ALU.bitwise_and).then_inc(yexp_ready, 1)
                dve.wait_ge(yexp_ready, (t + 1).n)
                if t.after(1):
                    dve.wait_ge(yround_ready, t.n)
                v.tensor_scalar(y_magic[:, :], y_exp[:, :], FP8_MIN_NORMAL, ROUND_TO_4_BITS,
                                ALU.max, ALU.mult).then_inc(magic_ready, 1)

            def quantise(t):
                dve.wait_ge(yround_ready, (t + 1).n)
                if t.after(2):
                    dve.wait_ge(f_done, (t - 1).n)
                v.tensor_scalar(xq[:, t.parity, :, :].rearrange("p c s -> p (c s)"), y_round[:, :],
                                FP8_MAX, -FP8_MAX, ALU.min, ALU.max).then_inc(xq_ready, 1)

            def shift(i, m, bank, done, added, added_ready, mx, mx_ready, sh, sh_ready, read):
                dve.wait_ge(done, (i + 1).n)
                v.tensor_tensor(added[:, :], bank[:, :], bias[:, m, :], ALU.add).then_inc(added_ready, 1)
                dve.wait_ge(added_ready, (i + 1).n)
                v.tensor_reduce(mx[:, :], heads(added[:, :]), AX.X, ALU.max).then_inc(mx_ready, 1)
                dve.wait_ge(mx_ready, (i + 1).n)
                if i.after(1):
                    dve.wait_ge(read, i.n)
                v.tensor_tensor(heads(sh[:, :]), heads(added[:, :]), per_head(mx[:, :]), ALU.subtract)\
                    .then_inc(sh_ready, 1)

            def state(i):
                dve.wait_ge(state_done, (i + 1).n)
                for n in range(2):
                    half = slice(n * G // 2, (n + 1) * G // 2)
                    last = v.tensor_tensor(
                        st_masked[:, half, :, :],
                        s_state[:, n, :].rearrange("p (g j w) -> p g j w", j=J, w=VW),
                        head_mask[:, None, :, None].to_broadcast([P, G // 2, J, VW]), ALU.mult)
                last.then_inc(masked_ready, 1)
                dve.wait_ge(masked_ready, (i + 1).n)
                v.tensor_reduce(st_step[:, :, :], st_masked[:, :, :, :].rearrange("p g j w -> p g w j"),
                                AX.X, ALU.add).then_inc(ststep_ready, 1)
                dve.wait_ge(ststep_ready, (i + 1).n)
                v.tensor_tensor(st_run[:, :, :], st_run[:, :, :], st_step[:, :, :], ALU.add)\
                    .then_inc(strun_ready, 1)
                dve.wait_ge(strun_ready, (i + 1).n)
                if i.after(1):
                    dve.wait_ge(a_done, i.n)
                v.tensor_tensor(st_seqs[:, (i + 1).parity, :, :, :],
                                st_run[:, :, None, :].to_broadcast([P, G, SEQS, VW]),
                                seq_mask[:, None, :, None].to_broadcast([P, G, SEQS, VW]), ALU.mult)\
                    .then_inc(stseqs_ready, 1)

            def mask_scores(i, c):
                dve.wait_ge(scores_done, i.n * 4 + c + 1)
                if c == 0 and i.after(1):
                    dve.wait_ge(a_done, i.n)
                v.tensor_tensor(att[:, 4 * c:4 * c + 4, :, :].rearrange("p g j s -> p (g j) s"),
                                s_ps[:, DM * (c % 2):DM * (c % 2 + 1)].rearrange("p (h s) -> p h s", s=TOK),
                                tri[:, None, :].to_broadcast([P, 4 * J, TOK]), ALU.mult)\
                    .then_inc(att_ready, 1)

            def body(i):
                t = i + 1
                if t.exists():
                    statistics(t)
                if i.exists():
                    shift(i, MK, k_ps, k_done, k_b, kb_ready, k_max, kmax_ready, k_shift, kshift_ready,
                          ke_ready)
                    shift(i, MQ, q_ps, q_done, q_b, qb_ready, q_max, qmax_ready, q_shift, qshift_ready,
                          qe_ready)
                    dve.wait_ge(ke_ready, (i + 1).n)
                    v.tensor_reduce(k_sum[:, :], heads(k_e[:, :]), AX.X, ALU.add).then_inc(ksum_ready, 1)
                    dve.wait_ge(ksum_ready, (i + 1).n)
                    v.reciprocal(k_rec[:, :], k_sum[:, :]).then_inc(krec_ready, 1)
                    dve.wait_ge(qe_ready, (i + 1).n)
                    if i.after(1):
                        dve.wait_ge(qheads_ready, i.n)
                    v.transpose(qT[:, :, :].rearrange("p g s -> p (g s)"), q_e[:, :]).then_inc(qT_ready, 1)
                    dve.wait_ge(v_done, (i + 1).n)
                    if i.after(1):
                        dve.wait_ge(vseqs_ready, i.n)
                    v.tensor_tensor(v_b[:, :], vo_ps[:, :], bias[:, MV, :], ALU.add).then_inc(vb_ready, 1)
                    dve.wait_ge(kn_ready, (i + 1).n)
                    if i.after(1):
                        dve.wait_ge(kseqs_ready, i.n * 4)
                    v.transpose(kT[:, :, :].rearrange("p g s -> p (g s)"), k_n[:, i.parity, :])\
                        .then_inc(kT_ready, 1)
                t = i + 1
                if t.exists():
                    normalise(t)
                t = i - 1
                if t.exists() and i.exists():
                    state(t)
                t = i - 1
                if t.exists():
                    dve.wait_ge(a_done, (t + 1).n)
                    for n in range(2):
                        a_n_ps = a_view[:, n, :].rearrange("p (m w) -> p m w", w=VW)
                        last = v.reciprocal(den_rec[:, n, :], a_n_ps[:, :, DH])
                    last.then_inc(rec_ready, 1)
                    dve.wait_ge(rec_ready, (t + 1).n)
                    if t.after(1):
                        dve.wait_ge(aT_done, t.n)
                    for n in range(2):
                        a_n_ps = a_view[:, n, :].rearrange("p (g b w) -> p g b w", b=SEQS, w=VW)
                        rec = den_rec[:, n, :].rearrange("p (g b) -> p g b", b=SEQS)
                        last = v.tensor_tensor(
                            a_n[:, :, n * G // 2:(n + 1) * G // 2, :].rearrange("p b g d -> p g b d"),
                            a_n_ps[:, :, :, 0:DH],
                            rec[:, :, :, None].to_broadcast([P, G // 2, SEQS, DH]), ALU.mult)
                    last.then_inc(an_ready, 1)
                if i.exists():
                    mask_scores(i, 0)
                    mask_scores(i, 1)
                t = i - 1
                if t.exists():
                    dve.wait_ge(ah_ready, (t + 1).n)
                    v.tensor_tensor(al[:, :, :].rearrange("p j s -> p (j s)"), aT_ps,
                                    ah[:, :, :].rearrange("p j s -> p (j s)"), ALU.subtract)\
                        .then_inc(al_ready, 1)
                if i.exists():
                    mask_scores(i, 2)
                    mask_scores(i, 3)
                t = i + 1
                if t.exists():
                    low_input(t)
                    magic(t)
                t = i - 1
                if t.exists():
                    dve.wait_ge(o_done, (t + 1).n)
                    dve.wait_ge(xres_ready, (t + 1).n)
                    if t.after(2):
                        dve.wait_ge(stored[t.parity], t.half * 16)
                    v.scalar_tensor_tensor(o_sb[:, t.parity, :], vo_ps[:, :], out_dn[:, :],
                                           x_res[:, t.parity, :], ALU.mult, ALU.add).then_inc(o_ready, 1)
                t = i + 1
                if t.exists():
                    quantise(t)

            def largest(m):
                dve.wait_ge(w_loaded[m], 16)
                v.tensor_reduce(amax[:, m:m + 1], staged[m], AX.XY, ALU.max,
                                apply_absolute_value=True).then_inc(amax_ready, 1)

            def powers(part):
                link(v.tensor_scalar(amax_all[:, part], amax_all[:, part], 1e-18, 1e18, ALU.max, ALU.min))
                link(v.tensor_scalar(w_top[:, part].bitcast(I32), amax_all[:, part].bitcast(I32), EXPONENT,
                                     None, ALU.bitwise_and))
                link(v.tensor_scalar(w_scale_dn[:, part], w_top[:, part], 2.0, None, ALU.mult))
                link(v.reciprocal(w_scale_up[:, part], w_scale_dn[:, part]))

            def low_parts(m):
                for c in range(KC):
                    n = turn.index(m) * KC + c
                    dve.wait_ge(wh_ready, n + 1)
                    v.scalar_tensor_tensor(w_lo[:, m, c, :], setup_banks[n % len(setup_banks)],
                                           w_mult[:, m:m + 1], w_hi[:, m, c, :], ALU.mult, ALU.subtract)\
                        .then_inc(wl_ready, 1)

            first = Step(0, 0)
            dve.wait_ge(m_loaded, 48)
            link(v.reciprocal(in_rec[:, :], scal[:, 1:2]))
            v.tensor_scalar(in_inv[:, :], in_rec[:, :], 1e30, -1e30, ALU.min, ALU.max)\
                .then_inc(in_inv_ready, 1)
            statistics(first)
            link(v.tensor_tensor(both_scales[:, :], scal[:, 1:2], scal[:, 2:3], ALU.mult))
            link(v.tensor_scalar(neg_scales[:, :], both_scales[:, :], -1.0, None, ALU.mult))
            link(v.tensor_tensor(abs_scales[:, :], both_scales[:, :], neg_scales[:, :], ALU.max))
            normalise(first)
            largest(MK)
            low_input(first)
            magic(first)
            largest(MQ)
            largest(MV)
            quantise(first)
            dve.wait_ge(amax_shared, 1)
            powers(slice(0, MO))
            v.tensor_copy(w_mult[:, 0:MO], w_scale_up[:, 0:MO]).then_inc(mult_ready, 1)
            dve.wait_ge(mult_ready, 1)
            largest(MO)
            low_parts(MK)
            largest(MF)
            low_parts(MQ)
            low_parts(MV)
            dve.wait_ge(amax_shared, 2)
            link(v.tensor_tensor(amax_all[:, MF:], amax_all[:, MF:], abs_scales[:, :], ALU.mult))
            powers(slice(MO, MATRICES))
            link(v.tensor_tensor(up_product[:, :], w_scale_up[:, MO:MF], w_scale_up[:, MV:MO], ALU.mult))
            link(v.tensor_tensor(out_up[:, :], up_product[:, :], w_scale_up[:, MF:], ALU.min))
            link(v.tensor_tensor(w_mult[:, MO:MF], out_up[:, :], w_scale_dn[:, MV:MO], ALU.mult))
            v.tensor_tensor(w_mult[:, MF:], both_scales[:, :], out_up[:, :], ALU.mult).then_inc(mult_ready, 1)
            link(v.reciprocal(out_dn[:, :], out_up[:, :]))
            dve.wait_ge(beta_exped, 1)
            link(v.tensor_tensor(q_exp_scale[:, :], exp_beta[:, :], w_scale_dn[:, MQ:MQ + 1], ALU.mult))
            link(v.tensor_tensor(k_exp_scale[:, :], exp_beta[:, :], w_scale_dn[:, MK:MK + 1], ALU.mult))
            dve.wait_ge(b_loaded, 16 * 5)
            for m in (MQ, MK, MV):
                link(v.tensor_scalar(bias[:, m, :], bias[:, m, :], w_scale_up[:, m:m + 1], None, ALU.mult))
            dve.wait_ge(mult_ready, 2)
            low_parts(MO)
            low_parts(MF)
            iterations(dve, body)

        @block.tensor
        def _(pe):
            mm = nc.tensor.matmul
            def a_col(g):
                return DM * (g // (G // 2)) + GW * (g % (G // 2))

            def project(bank, m):
                for c in range(KC):
                    mm(bank[:, :], xh[:, c, :], w_hi[:, m, c, :], start=(c == 0), stop=False)
                    mm(bank[:, :], xh[:, c, :], w_lo[:, m, c, :], start=False, stop=False)
                    last = mm(bank[:, :], xl[:, c, :], w_hi[:, m, c, :], start=False, stop=(c == KC - 1))
                return last

            def scores(i, c):
                pe.wait_ge(kseqs_ready, i.n * 4 + c + 1)
                if c < 2:
                    if i.after(1):
                        pe.wait_ge(masked_ready, i.n)
                else:
                    pe.wait_ge(att_ready, i.n * 4 + c - 1)
                for gg in range(4):
                    g = 4 * c + gg
                    last = mm(s_ps[:, DM * (c % 2) + P * gg:DM * (c % 2) + P * (gg + 1)],
                              k_seqs[:, g, :, :], q_heads[:, i.parity, g, :, :], start=True, stop=True)
                last.then_inc(scores_done, 1)

            def body(i, low_part=True):
                if i.exists():
                    pe.wait_ge(xh_ready, (i + 1).n)
                    pe.wait_ge(xl_ready, (i + 1).n)
                    if i.after(1):
                        pe.wait_ge(kb_ready, i.n)
                    project(k_ps, MK).then_inc(k_done, 1)
                t = i - 1
                if t.exists() and i.exists():
                    pe.wait_ge(kn_ready, (t + 1).n)
                    pe.wait_ge(vseqs_ready, (t + 1).n)
                    pe.wait_ge(att_ready, (t + 1).n * 4)
                    pe.sem_inc(pe_waited, 1)
                    for g in range(G):
                        col = DM * (g // (G // 2)) + J * VW * (g % (G // 2))
                        for b in range(SEQS):
                            rows = slice(TOK * b, TOK * (b + 1))
                            last = mm(s_ps[rows, col:col + J * VW], k_n[rows, t.parity, TOK * g:TOK * (g + 1)],
                                      v_seqs[rows, t.parity, J * g:J * (g + 1), b, :], start=True, stop=True)
                    last.then_inc(state_done, 1)
                if i.exists():
                    if i.after(1):
                        pe.wait_ge(qb_ready, i.n)
                    project(q_ps, MQ).then_inc(q_done, 1)
                    if i.after(2):
                        pe.wait_ge(o_ready, (i - 1).n)
                    project(vo_ps, MV).then_inc(v_done, 1)
                t = i - 1
                if t.exists():
                    if t.after(1):
                        pe.wait_ge(stseqs_ready, t.n)
                        pe.wait_ge(al_ready, t.n)
                    pe.wait_ge(qheads_ready, (t + 1).n)
                    for g in range(G):
                        for j in range(J):
                            mm(a_ps[TOK * j:TOK * (j + 1), a_col(g):a_col(g) + GW],
                               q_heads[:, t.parity, g, j, :], st_seqs[:, t.parity, g, :, :],
                               start=(g % (G // 2) == 0), stop=False, skip_group_check=True)
                    pe.wait_ge(att_ready, (t + 1).n * 4)
                    pe.wait_ge(vseqs_ready, (t + 1).n)
                    for g in range(G):
                        for j in range(J):
                            last = mm(a_ps[TOK * j:TOK * (j + 1), a_col(g):a_col(g) + GW], att[:, g, j, :],
                                      v_seqs[:, t.parity, J * g + j, :, :], start=False, stop=True,
                                      skip_group_check=True)
                    last.then_inc(a_done, 1)
                    pe.wait_ge(xq_ready, (t + 1).n)
                    if i.exists():
                        pe.wait_ge(vb_ready, (i + 1).n)
                    else:
                        pe.wait_ge(o_ready, t.n)
                    for c in range(KC):
                        last = mm(vo_ps[:, :], xq[:, t.parity, c, :], w_hi[:, MF, c, :], start=(c == 0),
                                  stop=False)
                        if low_part:
                            last = mm(vo_ps[:, :], xq[:, t.parity, c, :], w_lo[:, MF, c, :], start=False,
                                      stop=False)
                    last.then_inc(f_done, 1)
                t = i + 1
                if t.exists():
                    pe.wait_ge(xn_ready, (t + 1).n)
                    if t.after(1):
                        pe.wait_ge(xl_ready, t.n)
                    for c in range(KC):
                        last = nc.tensor.transpose(t_ps[:, P * c:P * (c + 1)], xn[:, P * c:P * (c + 1)], ident)
                    last.then_inc(xT_done, 1)
                if i.exists():
                    pe.wait_ge(qheads_ready, (i + 1).n)
                    scores(i, 0)
                    scores(i, 1)
                t = i - 1
                if t.exists():
                    pe.wait_ge(an_ready, (t + 1).n)
                    for b in range(SEQS):
                        last = nc.tensor.transpose(
                            aT_ps.rearrange("p (j b s) -> p b j s", b=SEQS, s=TOK)[:, b],
                            a_n[:, b, :, :].rearrange("p g d -> p (g d)"), ident)
                    last.then_inc(aT_done, 1)
                if i.exists():
                    scores(i, 2)
                    scores(i, 3)
                if t.exists():
                    pe.wait_ge(ah_ready, (t + 1).n)
                    pe.wait_ge(al_ready, (t + 1).n)
                    for j in range(J):
                        mm(vo_ps[:, :], ah[:, j, :], w_hi[:, MO, j, :], start=False, stop=False)
                        mm(vo_ps[:, :], ah[:, j, :], w_lo[:, MO, j, :], start=False, stop=False)
                        last = mm(vo_ps[:, :], al[:, j, :], w_hi[:, MO, j, :], start=False, stop=(j == J - 1))
                    last.then_inc(o_done, 1)

            pe.wait_ge(c_loaded, 16)
            body(Step(0, -1))
            for k, m in enumerate(turn):
                if m == MO:
                    pe.wait_ge(wo_ordered, 1)
                else:
                    pe.wait_ge(w_loaded[m], 16)
                for c in range(KC):
                    n = k * KC + c
                    if n >= len(setup_banks):
                        pe.wait_ge(wl_ready, n + 1 - len(setup_banks))
                    for oc in range(KC):
                        src = (wo_kept if m == MO else staged[m])[:, oc, c * P:(c + 1) * P]
                        last = nc.tensor.transpose(
                            setup_banks[n % len(setup_banks)][:, oc * P:(oc + 1) * P], src, ident)
                    last.then_inc(wt_done, 1)
            pe.wait_ge(wl_ready, chunks)
            body(Step(0, 0))
            pe.wait_ge(lo_shared, 1)
            any_low = pe.value_load(lo_total[0:1, 0:1].bitcast(I32), min_val=0, max_val=0x7FFFFFFF)
            with pe.If(any_low == 0):
                iterations(pe, lambda i: body(i, low_part=False), first=1)
            with pe.Else():
                iterations(pe, body, first=1)


_INS = ["L0_attn_x", "L0_attn_Wq", "L0_attn_bq", "L0_attn_Wk", "L0_attn_bk", "L0_attn_Wv", "L0_attn_bv",
        "L0_attn_Wo", "L0_attn_bo", "L0_attn_beta", "L0_ffn_weight_fp8", "L0_ffn_bias",
        "L0_ffn_input_scale", "L0_ffn_weight_scale"]


def constants():
    c = np.zeros((P, C_ALL), np.float32)
    p = np.arange(P)
    c[:, C_ID:C_ID + P] = np.eye(P)
    c[:, C_HEAD:C_HEAD + J] = (p[:, None] % TOK) // DH == np.arange(J)
    c[:, C_SEQ:C_SEQ + SEQS] = p[:, None] // TOK == np.arange(SEQS)
    c[:, C_TRI:C_TRI + TOK] = p[:, None] % TOK <= np.arange(TOK)
    return c


def kernel(**inputs):
    import concourse.bacc as bacc
    from concourse.bass_utils import run_bass_kernel_spmd

    nc = bacc.Bacc("TRN2", target_bir_lowering=False, num_devices=1)
    arrays = {name: np.ascontiguousarray(inputs[name]) for name in _INS}
    arrays["const"] = constants()
    args = [nc.dram_tensor(name, a.shape, F32, kind="ExternalInput").ap() for name, a in arrays.items()]
    out = nc.dram_tensor("out", (SEQS, LEN, DM), F32, kind="ExternalOutput").ap()
    build(nc, *args, out)
    r = run_bass_kernel_spmd(nc, [arrays], core_ids=[0])
    return r.results[0]["out"]
```
